# Optimizing a Trainium2 kernel written in Bass

```python
import numpy as np
import jax
import jax.numpy as jnp

def _softmax(x, axis=-1):
    return jax.nn.softmax(x, axis=axis)

def _gelu(x):
    return jax.nn.gelu(x, approximate=True)

def _silu(x):
    return jax.nn.silu(x)

def _sigmoid(x):
    return jax.nn.sigmoid(x)

def _layernorm(x, axis=-1, eps=1e-05):
    m = jnp.mean(x, axis=axis, keepdims=True)
    v = jnp.var(x, axis=axis, keepdims=True)
    return (x - m) / jnp.sqrt(v + eps)

def _scatter_add(tgt, idx, src, axis=0):
    return tgt.at[idx].add(src)

def _segment_sum(src, seg, n):
    return jax.ops.segment_sum(src, seg, n)
kernel_name = 'mk_sandwich_d1_jaxref_r8_423e12'

def setup_inputs(seed: int=0):
    np.random.seed(seed)
    _w = jnp.asarray

    def _L0_attn_setup():
        import math
        import jax, jax.numpy as jnp
        import numpy as np
        B, N, D = (4, 512, 128)
        H, M = (16, 64)
        HD = D // H
        EPS = 1e-06

        def favor_features(data, proj):
            hd = data.shape[-1]
            m = proj.shape[0]
            dn = data / math.sqrt(hd)
            norm_sq = 0.5 * jnp.sum(dn * dn, axis=-1, keepdims=True)
            comb = jnp.einsum('bhnd,md->bhnm', dn, proj) - norm_sq
            comb = comb - jnp.max(comb, axis=-1, keepdims=True)
            return jnp.exp(comb) / math.sqrt(m) + EPS
        key = jax.random.key(seed)
        ks = jax.random.split(key, 6)
        x = jax.random.normal(ks[0], (B, N, D), dtype=jnp.float32)
        qkv_w = jax.random.normal(ks[1], (3 * D, D), dtype=jnp.float32) * (1.0 / math.sqrt(D))
        qkv_b = jnp.zeros((3 * D,), dtype=jnp.float32)
        proj_w = jax.random.normal(ks[2], (D, D), dtype=jnp.float32) * (1.0 / math.sqrt(D))
        proj_b = jnp.zeros((D,), dtype=jnp.float32)
        pm = jax.random.normal(ks[3], (M, HD), dtype=jnp.float32)
        pm = pm / jnp.linalg.norm(pm, axis=-1, keepdims=True)
        return {'x': x, 'qkv_w': qkv_w, 'qkv_b': qkv_b, 'proj_w': proj_w, 'proj_b': proj_b, 'projection_matrix': pm}
    _L0_attn_in = _L0_attn_setup()

    def _L0_ffn_setup():
        import jax, jax.numpy as jnp
        import numpy as np
        import math
        BETA = 0.9
        THRESHOLD = 1.0
        NUM_STEPS = 5
        ALPHA = 2.0

        @jax.custom_vjp
        def spike_fn(u):
            return (u > 0).astype(u.dtype)

        def _spike_fwd(u):
            return (spike_fn(u), u)

        def _spike_bwd(u, g):
            s = jnp.pi / 2.0 * ALPHA * u
            return (g * (ALPHA / 2.0) / (1.0 + s * s),)
        spike_fn.defvjp(_spike_fwd, _spike_bwd)
        key = jax.random.key(seed)
        k1, k2, k3 = jax.random.split(key, 3)
        n_embd = 128
        x = jax.random.normal(k1, (4, 256, n_embd), dtype=jnp.float32)
        W_fc = jax.random.normal(k2, (4 * n_embd, n_embd), dtype=jnp.float32) / math.sqrt(n_embd)
        W_proj = jax.random.normal(k3, (n_embd, 4 * n_embd), dtype=jnp.float32) / math.sqrt(4 * n_embd)
        return {'x': x, 'W_fc': W_fc, 'W_proj': W_proj}
    _L0_ffn_in = _L0_ffn_setup()
    _d = {'L0_attn_x': _L0_attn_in['x'], 'L0_attn_qkv_w': _L0_attn_in['qkv_w'], 'L0_attn_qkv_b': _L0_attn_in['qkv_b'], 'L0_attn_proj_w': _L0_attn_in['proj_w'], 'L0_attn_proj_b': _L0_attn_in['proj_b'], 'L0_attn_projection_matrix': _L0_attn_in['projection_matrix'], 'L0_ffn_W_fc': _L0_ffn_in['W_fc'], 'L0_ffn_W_proj': _L0_ffn_in['W_proj']}
    _x0 = _d['L0_attn_x']
    _d['L0_attn_x'] = jax.random.normal(jax.random.fold_in(jax.random.key(seed), 1), (16, 256, 128), dtype=_x0.dtype)
    del _x0
    return _d

def reference(L0_attn_x, L0_attn_qkv_w, L0_attn_qkv_b, L0_attn_proj_w, L0_attn_proj_b, L0_attn_projection_matrix, L0_ffn_W_fc, L0_ffn_W_proj):

    def _L0_attn_ref(x, qkv_w, qkv_b, proj_w, proj_b, projection_matrix):
        import math
        import jax, jax.numpy as jnp
        import numpy as np
        B, N, D = (4, 512, 128)
        H, M = (16, 64)
        HD = D // H
        EPS = 1e-06

        def favor_features(data, proj):
            hd = data.shape[-1]
            m = proj.shape[0]
            dn = data / math.sqrt(hd)
            norm_sq = 0.5 * jnp.sum(dn * dn, axis=-1, keepdims=True)
            comb = jnp.einsum('bhnd,md->bhnm', dn, proj) - norm_sq
            comb = comb - jnp.max(comb, axis=-1, keepdims=True)
            return jnp.exp(comb) / math.sqrt(m) + EPS
        b, n, d = x.shape
        qkv = x @ qkv_w.T + qkv_b
        qkv = qkv.reshape(b, n, 3, H, HD)
        qkv = jnp.transpose(qkv, (2, 0, 3, 1, 4))
        q, k, v = (qkv[0], qkv[1], qkv[2])
        q_p = favor_features(q, projection_matrix)
        k_p = favor_features(k, projection_matrix)
        kv = jnp.einsum('bhnm,bhnv->bhmv', k_p, v)
        out = jnp.einsum('bhnm,bhmv->bhnv', q_p, kv)
        k_sum = jnp.sum(k_p, axis=2)
        normalizer = jnp.einsum('bhnm,bhm->bhn', q_p, k_sum)[..., None]
        out = out / (normalizer + EPS)
        out = jnp.transpose(out, (0, 2, 1, 3)).reshape(b, n, d)
        return out @ proj_w.T + proj_b

    def _L0_ffn_ref(x, W_fc, W_proj):
        import jax, jax.numpy as jnp
        import numpy as np
        import math
        BETA = 0.9
        THRESHOLD = 1.0
        NUM_STEPS = 5
        ALPHA = 2.0

        @jax.custom_vjp
        def spike_fn(u):
            return (u > 0).astype(u.dtype)

        def _spike_fwd(u):
            return (spike_fn(u), u)

        def _spike_bwd(u, g):
            s = jnp.pi / 2.0 * ALPHA * u
            return (g * (ALPHA / 2.0) / (1.0 + s * s),)
        spike_fn.defvjp(_spike_fwd, _spike_bwd)
        h = jnp.square(jax.nn.relu(jnp.einsum('bsd,fd->bsf', x, W_fc)))
        y = jnp.einsum('bsf,df->bsd', h, W_proj)

        def step(mem, _):
            reset = jax.lax.stop_gradient(spike_fn(mem - THRESHOLD))
            mem_new = BETA * mem + y - reset * THRESHOLD
            spk = spike_fn(mem_new - THRESHOLD)
            return (mem_new, spk)
        mem0 = jnp.zeros_like(y)
        _, spks = jax.lax.scan(step, mem0, None, length=NUM_STEPS)
        return jnp.sum(spks, axis=0) / NUM_STEPS
    x = L0_attn_x
    x = x + _layernorm(_L0_attn_ref(_layernorm(x, axis=-1), L0_attn_qkv_w, L0_attn_qkv_b, L0_attn_proj_w, L0_attn_proj_b, L0_attn_projection_matrix), axis=-1)
    x = x + _layernorm(_L0_ffn_ref(_layernorm(x, axis=-1), L0_ffn_W_fc, L0_ffn_W_proj), axis=-1)
    return x

_drawn_inputs = setup_inputs


def setup_inputs(seed=0):
    import zlib

    import numpy as np

    out = dict(_drawn_inputs(seed))
    spreads = {'L0_attn_qkv_b': (0.0, 0.1), 'L0_attn_proj_b': (0.0, 0.1)}
    factors = {}
    for name, (base, spread) in spreads.items():
        noise = np.random.default_rng([zlib.crc32(name.encode()), seed]).standard_normal(out[name].shape)
        drawn = base * np.exp(spread * noise) if base else spread * noise
        out[name] = jnp.asarray(drawn.astype(out[name].dtype))
    for name, factor in factors.items():
        out[name] = (out[name] * factor).astype(out[name].dtype)
    return out
```

```python
from contextlib import ExitStack

import concourse.bass as bass
from concourse import mybir

F32 = mybir.dt.float32
F16 = mybir.dt.float16
BF16 = mybir.dt.bfloat16
ALU = mybir.AluOpType
ACT = mybir.ActivationFunctionType
AX_X = mybir.AxisListType.X

P = 128
EPS_LN = 1e-5
EPS_FAVOR = 1e-6
BETA = 0.9
NUM_STEPS = 5
SPLIT_SCALE = 64.0


def spike_thresholds():
    def spikes(y):
        m, n = 0.0, 0
        for _ in range(NUM_STEPS):
            m = BETA * m + y - (1.0 if m > 1.0 else 0.0)
            n += m > 1.0
        return n

    edges = []
    for n in range(1, NUM_STEPS + 1):
        low, high = 0.0, 4.0
        for _ in range(80):
            mid = (low + high) / 2
            low, high = (low, mid) if spikes(mid) >= n else (mid, high)
        edges.append(high)
    return edges


def sandwich_kernel(nc, x, qkv_w, qkv_b, proj_w, proj_b, pm, w_fc, w_proj, const, indicator, out):
    NB, N, D = x.shape
    M, HD = pm.shape
    H = D // HD
    FF = w_fc.shape[0]
    NT = N // P
    NG = P // 32
    HG = H // NG
    GW = HG * M
    NP = H // 2
    VW = HD + 1
    FC = FF // P
    HM = H * M
    EXP_SCALE = 1.0 / (SPLIT_SCALE * SPLIT_SCALE * float(HD) ** 0.5)
    EPS8 = 8.0 * EPS_FAVOR
    assert NT == 2 and HM == 1024 and FF == 512 and M == 64 and NB % 2 == 0
    thresholds = spike_thresholds()

    x_v = x.rearrange("b (t p) d -> b p t d", p=P)
    out_v = out.rearrange("b (t p) d -> b p t d", p=P)

    with ExitStack() as ctx:
        def sb(name, shape, dt=F32):
            return ctx.enter_context(nc.sbuf_tensor(name, shape, dt))

        def sem(name):
            return ctx.enter_context(nc.semaphore(name))

        cst = sb("cst", [P, P + NG + 2])
        ident = cst[:, 0:P]
        head_mask = cst[:, P:P + HG]
        ident_bf = sb("ident_bf", [P, P], BF16)
        ind = sb("ind", [P, HM], F16)
        eps8 = sb("eps8", [P, P])
        neg_half = sb("neg_half", [P, NT])
        w_raw = sb("w_raw", [P, 3 + 1 + FC + FC, P])
        pm16 = sb("pm16", [M, 4 * HG, HD])
        pm_raw = sb("pm_raw", [M, HD])
        bq_raw = sb("bq_raw", [P, 2])
        bq = sb("bq", [P, 2])
        bv = sb("bv", [P, NT, D])
        bp = sb("bp", [P, NT, D])
        wqk_t = sb("wqk_t", [P, 2, D])
        wv_t = sb("wv_t", [P, D])
        wp_t = sb("wp_t", [P, D])
        wfc_t = sb("wfc_t", [P, FC, P])
        wpr_t = sb("wpr_t", [P, FC, D])
        pf = sb("pf", [P, HG, M])
        pf_hi = sb("pf_hi", [P, HG, M], F16)
        pf_lo = sb("pf_lo", [P, HG, M], F16)
        pst_a = sb("pst_a", [P, HG * M], F16)
        pst = sb("pst", [P, HG * M], F16)

        xin = [sb(f"xin{i}", [P, NT, D]) for i in range(2)]
        xres = sb("xres", [P, NT, D])
        xn = sb("xn", [P, NT, D])
        xn_t = sb("xn_t", [P, N])
        hi = sb("hi", [P, 2, N], F16)
        lo = sb("lo", [P, 2, N], F16)
        stack = [sb(f"stack{i}", [P, NG, 2, N], F16) for i in range(2)]
        vaug = [sb(f"vaug{i}", [P, NT, H, VW]) for i in range(2)]
        nmax_q = sb("nmax_q", [P, NT, H])
        nmax_k = sb("nmax_k", [P, NT, H])
        rem_q = sb("rem_q", [P, NT, H])
        rem_k = sb("rem_k", [P, NT, H])
        parts_q = sb("parts_q", [P, NT, P], BF16)
        parts_k = sb("parts_k", [P, NT, P], BF16)
        parts_qt = sb("parts_qt", [P, N], BF16)
        parts_kt = sb("parts_kt", [P, N], BF16)
        ek = sb("ek", [P, NT, HM])
        eq_t = sb("eq_t", [P, NP, N])
        kvb = sb("kvb", [P, NP, 2 * VW])
        den = sb("den", [P, NT * H])
        rden = sb("rden", [P, NT * H])
        att = sb("att", [P, NT * H, HD])
        att_t = sb("att_t", [P, N])
        a_sb = sb("a_sb", [P, NT, D])
        x1 = [sb(f"x1_{i}", [P, NT, D]) for i in range(2)]
        x1n = sb("x1n", [P, NT, D])
        xn2 = sb("xn2", [P, NT, D])
        xn2_t = sb("xn2_t", [P, N])
        relu = sb("relu", [P, FC, N])
        hsq = sb("hsq", [P, FC, N])
        cnt = [sb(f"cnt{i}", [P, NT * D]) for i in range(2)]
        cn = sb("cn", [P, NT, D])
        xo = sb("xo", [P, NT, D])
        st = [sb(f"st{k}", [P, NT, 6]) for k in range(4)]
        mv = [sb(f"mv{k}", [P, NT, 2]) for k in range(4)]
        var = [sb(f"var{k}", [P, NT]) for k in range(4)]
        nmean = [sb(f"nmean{k}", [P, NT]) for k in range(4)]
        rstd = [sb(f"rstd{k}", [P, NT]) for k in range(4)]

        wide = [ctx.enter_context(nc.psum_tensor(f"wide{i}", [P, HM], F32)) for i in range(3)]
        m0 = ctx.enter_context(nc.psum_tensor("m0", [P, 512], F32))
        m1 = ctx.enter_context(nc.psum_tensor("m1", [P, 512], F32))

        s_settled = [sem("s_settled_dve"), sem("s_settled_pool")]
        s_const = sem("s_const")
        s_zero = sem("s_zero")
        s_wtr = sem("s_wtr")
        s_wcopy = sem("s_wcopy")
        s_prep = sem("s_prep")
        s_idbf = sem("s_idbf")
        s_pmrep = sem("s_pmrep")
        s_xin = [sem("s_xin0"), sem("s_xin1")]
        s_xres = sem("s_xres")
        s_stat = [sem(f"s_stat{k}") for k in range(4)]
        s_mv = [sem(f"s_mv{k}") for k in range(4)]
        s_var = [sem(f"s_var{k}") for k in range(4)]
        s_rstd = [sem(f"s_rstd{k}") for k in range(4)]
        s_xn = sem("s_xn")
        s_xt = sem("s_xt")
        s_xnt = sem("s_xnt")
        s_qk = sem("s_qk")
        s_hi = sem("s_hi")
        s_lo = sem("s_lo")
        s_stack = [sem("s_stack0"), sem("s_stack1")]
        s_v = sem("s_v")
        s_vsb = sem("s_vsb")
        s_cq = sem("s_cq")
        s_ck = sem("s_ck")
        s_maxq = sem("s_maxq")
        s_maxk = sem("s_maxk")
        s_spq = sem("s_spq")
        s_spk = sem("s_spk")
        s_ptq = sem("s_ptq")
        s_ptk = sem("s_ptk")
        s_ptq_sb = sem("s_ptq_sb")
        s_ptk_sb = sem("s_ptk_sb")
        s_qt = sem("s_qt")
        s_ksub = sem("s_ksub")
        s_expq = sem("s_expq")
        s_expk = sem("s_expk")
        s_kv = sem("s_kv")
        s_kvb = sem("s_kvb")
        s_out = sem("s_out")
        s_den = sem("s_den")
        s_rden = sem("s_rden")
        s_att = sem("s_att")
        s_attt = sem("s_attt")
        s_attt_sb = sem("s_attt_sb")
        s_proj = sem("s_proj")
        s_a = sem("s_a")
        s_x1n = sem("s_x1n")
        s_x1 = sem("s_x1")
        s_xn2 = sem("s_xn2")
        s_x2t = sem("s_x2t")
        s_xn2t = sem("s_xn2t")
        s_ff1 = sem("s_ff1")
        s_relu = sem("s_relu")
        s_hsq = sem("s_hsq")
        s_y = sem("s_y")
        s_cnt = sem("s_cnt")
        s_cn = sem("s_cn")
        s_xo = sem("s_xo")
        s_store = sem("s_store")

        def wait(eng, s, value):
            if not isinstance(value, int) or value > 0:
                eng.wait_ge(s, value)

        def settle(eng):
            eng.sem_inc(s_settled[eng is nc.gpsimd], 1)

        class Slot:

            def __init__(self, half, off):
                self.half, self.base, self.off = half, half * 2, off

            def seq(self, k):
                return self.base + (self.off - k)

            def par(self, k):
                return (self.off - k) % 2

            def round(self, k):
                return self.half + (self.off - k - self.par(k)) // 2

            def active(self, k):
                return not isinstance(self.base, int) or 0 <= self.seq(k) < NB

        STAGES = 5
        PEELED = STAGES + 1
        LAST = NB + STAGES - 1

        def slots(eng, body):
            for t in range(PEELED):
                body(Slot(t // 2, t % 2))
            with eng.Fori(PEELED // 2, NB // 2) as i:
                for off in range(2):
                    body(Slot(i, off))
            for t in range(NB, LAST):
                body(Slot(t // 2, t % 2))

        def done(value):
            return min(value, NB) if isinstance(value, int) else value

        block = ctx.enter_context(nc.Block())

        N_CONST = 12

        @block.sync
        def _(sp):
            sp.dma_start(cst[:, :], const).then_inc(s_const, 16)
            sp.dma_start(w_raw[:, 0:3, :], qkv_w.rearrange("(c p) d -> p c d", p=P)).then_inc(s_const, 16)
            sp.dma_start(pm_raw[:, :], pm).then_inc(s_const, 16)
            sp.dma_start(w_raw[:, 3, :], proj_w).then_inc(s_const, 16)
            sp.dma_start(w_raw[:, 4:4 + FC, :], w_fc.rearrange("(c p) d -> p c d", p=P)).then_inc(s_const, 16)
            sp.dma_start(w_raw[:, 4 + FC:, :], w_proj.rearrange("d (c f) -> d c f", c=FC)).then_inc(s_const, 16)
            with nc.allow_non_contiguous_dma(reason="two short bias columns"):
                sp.dma_start(bq_raw[:, :], qkv_b[0:2 * D].rearrange("(c p) -> p c", p=P)).then_inc(s_const, 16)
            sp.dma_start(ind[:, :], indicator).then_inc(s_const, 16)
            for t in range(NT):
                sp.dma_start(bv[:, t, :], qkv_b[2 * D:3 * D].rearrange("(a d) -> a d", a=1).broadcast_to([P, D])).then_inc(s_const, 16)
                sp.dma_start(bp[:, t, :], proj_b.rearrange("(a d) -> a d", a=1).broadcast_to([P, D])).then_inc(s_const, 16)

            def body(s):
                if s.active(0):
                    b, p = s.seq(0), s.par(0)
                    wait(sp, s_xn, 2 * (b - 1))
                    sp.dma_start(xin[p][:, :, :], x_v[b]).then_inc(s_xin[p], 16)
                if s.active(3):
                    b = s.seq(3)
                    wait(sp, s_x1, b)
                    sp.dma_start(xres[:, :, :], x_v[b]).then_inc(s_xres, 16)
                if s.active(1):
                    b, p = s.seq(1), s.par(1)
                    wait(sp, s_hi, 2 * b + 2)
                    wait(sp, s_qt, 2 * (b - 1))
                    wait(sp, s_ck, 2 * (b - 1))
                    for g in range(NG):
                        for r in range(2):
                            sp.dma_start(stack[p][32 * r:32 * r + 32, g, :, :],
                                         hi[32 * g:32 * g + 32, :, :]).then_inc(s_stack[p], 16)
                    wait(sp, s_lo, 2 * b + 2)
                    for g in range(NG):
                        for r in range(2, 4):
                            sp.dma_start(stack[p][32 * r:32 * r + 32, g, :, :],
                                         lo[32 * g:32 * g + 32, :, :]).then_inc(s_stack[p], 16)
                if s.active(4):
                    b = s.seq(4)
                    wait(sp, s_xo, b + 1)
                    sp.dma_start(out_v[b], xo[:, :, :]).then_inc(s_store, 16)

            slots(sp, body)
            sp.wait_ge(s_store, 16 * NB)

        @block.gpsimd
        def _(pool):
            pool.memset(parts_q[:, :, :], 0.0).then_inc(s_zero, 1)
            pool.memset(parts_k[:, :, :], 0.0).then_inc(s_zero, 1)
            pool.memset(kvb[:, :, :], 0.0).then_inc(s_zero, 1)
            pool.memset(eps8[:, :], EPS8).then_inc(s_zero, 1)
            pool.memset(neg_half[:, :], -0.5).then_inc(s_zero, 1)
            for i in range(2):
                pool.memset(vaug[i][:, :, :, HD:VW], 1.0).then_inc(s_zero, 1)
            pool.wait_ge(s_zero, 7)

            def inv_std(k, b, eps, last_readers):
                for sm, value in last_readers:
                    wait(pool, sm, value)
                pool.wait_ge(s_mv[k], 2 * b + 2)
                settle(pool)
                pool.tensor_scalar(var[k][:, :], mv[k][:, :, 1], eps, None, ALU.add).then_inc(s_var[k], 1)
                pool.tensor_scalar(nmean[k][:, :], mv[k][:, :, 0], -1.0, None, ALU.mult).then_inc(s_var[k], 1)
                pool.wait_ge(s_var[k], 2 * b + 2)
                pool.tensor_tensor(rstd[k][:, :], var[k][:, :], neg_half[:, :], ALU.pow).then_inc(s_rstd[k], 1)
                pool.wait_ge(s_rstd[k], b + 1)

            def normalize(k, t, dst, src, done_sem):
                settle(pool)
                pool.tensor_scalar(dst, src, nmean[k][:, t:t + 1], rstd[k][:, t:t + 1], ALU.add,
                                   ALU.mult).then_inc(done_sem, 1)

            def split(nm, rem, parts, lo_t, hi_t, s_split, first):
                n = nm[:, lo_t:hi_t, :]
                r = rem[:, lo_t:hi_t, :]
                a = [parts[:, lo_t:hi_t, H * i:H * (i + 1)] for i in range(3)]
                settle(pool)
                pool.tensor_copy(a[0], n).then_inc(s_split, 1)
                pool.wait_ge(s_split, first + 1)
                pool.tensor_tensor(r, n, a[0], ALU.subtract).then_inc(s_split, 1)
                pool.wait_ge(s_split, first + 2)
                settle(pool)
                pool.tensor_copy(a[1], r).then_inc(s_split, 1)
                pool.wait_ge(s_split, first + 3)
                pool.tensor_tensor(a[2], r, a[1], ALU.subtract).then_inc(s_split, 1)

            def body(s):
                if s.active(0):
                    b, p = s.seq(0), s.par(0)
                    inv_std(0, b, EPS_LN, [])
                    wait(pool, s_xt, b)
                    for t in range(NT):
                        normalize(0, t, xn[:, t, :], xin[p][:, t, :], s_xn)
                if s.active(2):
                    b = s.seq(2)
                    pool.wait_ge(s_maxq, 2 * b + 2)
                    wait(pool, s_ptq, b)
                    split(nmax_q, rem_q, parts_q, 0, NT, s_spq, 4 * b)
                if s.active(4):
                    b = s.seq(4)
                    pool.wait_ge(s_relu, b + 1)
                    wait(pool, s_y, b)
                    for c in range(0, FC, 2):
                        pool.tensor_tensor(hsq[:, c:c + 2, :], relu[:, c:c + 2, :], relu[:, c:c + 2, :],
                                           ALU.mult).then_inc(s_hsq, 1)
                if s.active(2):
                    b = s.seq(2)
                    for t in range(NT):
                        pool.wait_ge(s_maxk, 2 * b + t + 1)
                        if t == 0:
                            wait(pool, s_ptk, 2 * b)
                        split(nmax_k, rem_k, parts_k, t, t + 1, s_spk, 8 * b + 4 * t)
                if s.active(3):
                    b, p = s.seq(3), s.par(3)
                    inv_std(1, b, EPS_LN, [])
                    for t in range(NT):
                        normalize(1, t, x1n[:, t, :], a_sb[:, t, :], s_x1n)
                    pool.wait_ge(s_x1n, 2 * b + 2)
                    pool.wait_ge(s_xres, 16 * (b + 1))
                    pool.tensor_tensor(x1[p][:, :, :], x1n[:, :, :], xres[:, :, :], ALU.add).then_inc(s_x1, 1)
                    inv_std(2, b, EPS_LN, [(s_x1, b + 1)])
                    wait(pool, s_x2t, b)
                    for t in range(NT):
                        normalize(2, t, xn2[:, t, :], x1[p][:, t, :], s_xn2)
                if s.active(4):
                    b, p = s.seq(4), s.par(4)
                    inv_std(3, b, EPS_LN * NUM_STEPS * NUM_STEPS, [])
                    for t in range(NT):
                        normalize(3, t, cn[:, t, :], cnt[0][:, t * D:(t + 1) * D], s_cn)
                    pool.wait_ge(s_cn, 2 * b + 2)
                    wait(pool, s_store, 16 * b)
                    pool.tensor_tensor(xo[:, :, :], cn[:, :, :], x1[p][:, :, :], ALU.add).then_inc(s_xo, 1)

            slots(pool, body)

        @block.scalar
        def _(act):
            act.wait_ge(s_const, 16 * N_CONST)
            act.activation(ident_bf[:, :], ident, ACT.Copy).then_inc(s_idbf, 1)
            act.activation(bq[:, :], bq_raw[:, :], ACT.Copy, scale=SPLIT_SCALE).then_inc(s_idbf, 1)
            act.wait_ge(s_wtr, 1)
            act.activation(wqk_t[:, :, :], wide[0][:, 0:2 * P].rearrange("p (c d) -> p c d", c=2), ACT.Copy,
                           scale=SPLIT_SCALE).then_inc(s_wcopy, 1)
            act.activation(wv_t[:, :], wide[0][:, 2 * P:3 * P], ACT.Copy).then_inc(s_wcopy, 1)
            act.activation(wp_t[:, :], wide[0][:, 3 * P:4 * P], ACT.Copy).then_inc(s_wcopy, 1)
            act.wait_ge(s_wtr, 2)
            act.activation(wfc_t[:, :, :], wide[1][:, 0:FC * P].rearrange("p (c d) -> p c d", c=FC),
                           ACT.Copy).then_inc(s_wcopy, 1)
            act.wait_ge(s_wtr, 3)
            act.activation(wpr_t[:, :, :], wide[2][:, 0:FC * P].rearrange("p (c d) -> p c d", c=FC),
                           ACT.Copy).then_inc(s_wcopy, 1)

            def body(s):
                if s.active(1):
                    b = s.seq(1)
                    act.wait_ge(s_xt, b + 1)
                    wait(act, s_v, b)
                    act.activation(xn_t[:, :], m0[:, 0:N], ACT.Copy).then_inc(s_xnt, 1)
                if s.active(4):
                    b = s.seq(4)
                    act.wait_ge(s_x2t, b + 1)
                    wait(act, s_ff1, b)
                    act.activation(xn2_t[:, :], m0[:, 0:N], ACT.Copy).then_inc(s_xn2t, 1)
                if s.active(3):
                    b = s.seq(3)
                    act.wait_ge(s_kv, b + 1)
                    wait(act, s_out, b)
                    for j in range(2):
                        act.activation(kvb[64 * j:64 * j + 64, :, VW * j:VW * j + VW],
                                       m1[64 * j:64 * j + 64, 0:NP * 2 * VW]
                                       .rearrange("p (n c) -> p n c", n=NP)[:, :, VW * j:VW * j + VW],
                                       ACT.Copy).then_inc(s_kvb, 1)
                if s.active(1):
                    b, p = s.seq(1), s.par(1)
                    act.wait_ge(s_qk, b + 1)
                    wait(act, s_stack[1 - p], 16 * 4 * NG * (s.round(1) + (p - 1) + 1))
                    for j in range(2):
                        act.activation(hi[:, j, :], m0[:, j * N:(j + 1) * N], ACT.Identity,
                                       bias=bq[:, j:j + 1]).then_inc(s_hi, 1)
                if s.active(4):
                    b = s.seq(4)
                    act.wait_ge(s_ff1, b + 1)
                    wait(act, s_hsq, 2 * b)
                    act.activation(relu[:, :, :], wide[2][:, :].rearrange("p (c n) -> p c n", c=FC),
                                   ACT.Relu).then_inc(s_relu, 1)
                if s.active(3):
                    b = s.seq(3)
                    act.wait_ge(s_attt, b + 1)
                    wait(act, s_proj, b)
                    act.activation(att_t[:, :], m1[:, 0:N], ACT.Copy).then_inc(s_attt_sb, 1)
                if s.active(2):
                    b = s.seq(2)
                    act.wait_ge(s_ptq, b + 1)
                    wait(act, s_qt, 2 * b)
                    act.activation(parts_qt[:, :], m0[:, 0:N // 2].bitcast(BF16), ACT.Copy).then_inc(s_ptq_sb, 1)
                    exp_q(s, 0)
                    exp_k(s, 0)
                    exp_q(s, 1)
                    exp_k(s, 1)

            def exp_q(s, j):
                b = s.seq(2)
                act.wait_ge(s_qt, 2 * b + j + 1)
                if j == 0:
                    wait(act, s_out, b)
                act.activation(eq_t[:, 4 * j:4 * j + 4, :], wide[2][:, :].rearrange("p (c n) -> p c n", c=4),
                               ACT.Exp, scale=EXP_SCALE).then_inc(s_expq, 1)

            def exp_k(s, t):
                b = s.seq(2)
                w = wide[1 - s.off % 2] if t == 0 else wide[s.off % 2]
                act.wait_ge(s_ptk, 2 * b + t + 1)
                wait(act, s_ksub, 2 * b + t - 1)
                act.activation(parts_kt[:, t * P:(t + 1) * P], m1[:, 0:P // 2].bitcast(BF16),
                               ACT.Copy).then_inc(s_ptk_sb, 1)
                act.wait_ge(s_ksub, 2 * b + t + 1)
                if t == 0:
                    wait(act, s_kv, b)
                act.activation(ek[:, t, :], w[:, :], ACT.Exp, scale=EXP_SCALE).then_inc(s_expk, 1)

            slots(act, body)

        @block.tensor
        def _(pe):
            pe.wait_ge(s_const, 16 * N_CONST)
            for c in range(4):
                mm = pe.transpose(wide[0][:, c * P:(c + 1) * P], w_raw[:, c, :], ident)
            mm.then_inc(s_wtr, 1)
            for c in range(FC):
                mm = pe.transpose(wide[1][:, c * P:(c + 1) * P], w_raw[:, 4 + c, :], ident)
            mm.then_inc(s_wtr, 1)
            for c in range(FC):
                mm = pe.transpose(wide[2][:, c * P:(c + 1) * P], w_raw[:, 4 + FC + c, :], ident)
            mm.then_inc(s_wtr, 1)
            pe.wait_ge(s_pmrep, 1)
            pe.matmul(m1[:, 0:M], pm16[:, :, :].rearrange("m r d -> m (r d)"), cst[0:M, 0:M], start=True,
                      stop=True).then_inc(s_wtr, 1)
            pe.wait_ge(s_wcopy, 5)
            pe.wait_ge(s_prep, 1)
            pe.wait_ge(s_idbf, 2)
            pe.wait_ge(s_zero, 7)

            def features(s, w, j, t, done_sem):
                p = s.par(2)
                for g in range(NG):
                    mm = pe.matmul(w[:, g * GW:(g + 1) * GW], stack[p][:, g, j, t * P:(t + 1) * P], pst[:, :],
                                   start=(g % 2 == 0), stop=False, skip_group_check=True)
                mm.then_inc(done_sem, 1)

            def features_t(s, half):
                p = s.par(2)
                for i in range(NP // 2):
                    pair = half * (NP // 2) + i
                    g, e = pair // 2, pair % 2
                    o = wide[2][:, i * N:(i + 1) * N]
                    pe.matmul(o, pst[:, e * P:(e + 1) * P], stack[p][:, g, 0, :],
                              start=(i % 2 == 0), stop=False, skip_group_check=True)
                    mm = pe.matmul(o, ind[:, pair * P:(pair + 1) * P], parts_qt[:, :], start=False,
                                   stop=True, skip_group_check=True)
                mm.then_inc(s_qt, 1)

            def body(s):
                u, v, z = wide[s.off % 2], wide[1 - s.off % 2], wide[2]
                if s.active(2):
                    b, p = s.seq(2), s.par(2)
                    pe.wait_ge(s_stack[p], 16 * 4 * NG * (s.round(2) + 1))
                    wait(pe, s_expk, 2 * b - 1)
                    features(s, u, 0, 0, s_cq)
                if s.active(1):
                    b = s.seq(1)
                    pe.wait_ge(s_xn, 2 * b + 2)
                    wait(pe, s_cnt, NUM_STEPS * s.seq(4))
                    wait(pe, s_ptq_sb, s.seq(2))
                    wait(pe, s_vsb, b)
                    for t in range(NT):
                        mm = pe.transpose(m0[:, t * P:(t + 1) * P], xn[:, t, :], ident)
                    mm.then_inc(s_xt, 1)
                if s.active(2):
                    b = s.seq(2)
                    wait(pe, s_expq, 2 * b)
                    features(s, z, 0, 1, s_cq)
                if s.active(4):
                    b = s.seq(4)
                    pe.wait_ge(s_xn2, 2 * b + 2)
                    wait(pe, s_xnt, done(s.seq(1) + 1))
                    wait(pe, s_cnt, NUM_STEPS * b)
                    for t in range(NT):
                        mm = pe.transpose(m0[:, t * P:(t + 1) * P], xn2[:, t, :], ident)
                    mm.then_inc(s_x2t, 1)
                if s.active(3):
                    b, p = s.seq(3), s.par(3)
                    pe.wait_ge(s_vsb, b + 1)
                    wait(pe, s_expk, 2 * b + 1)
                    ones = m1[:, 0:NP * 2 * VW]
                    for t in range(NT):
                        pe.matmul(ones, eps8[:, :], vaug[p][:, t, :, :].rearrange("p h c -> p (h c)"),
                                  start=(t == 0), stop=False, skip_group_check=True)
                    for t in range(NT):
                        if t == 1:
                            pe.wait_ge(s_expk, 2 * b + 2)
                        for n in range(NP):
                            mm = pe.matmul(m1[:, n * 2 * VW:(n + 1) * 2 * VW], ek[:, t, n * P:(n + 1) * P],
                                           vaug[p][:, t, 2 * n:2 * n + 2, :].rearrange("p h c -> p (h c)"),
                                           start=False, stop=True, skip_group_check=True)
                    mm.then_inc(s_kv, 1)
                if s.active(2):
                    b = s.seq(2)
                    wait(pe, s_expk, 2 * b)
                    features(s, v, 1, 0, s_ck)
                if s.active(1):
                    b = s.seq(1)
                    pe.wait_ge(s_xnt, b + 1)
                    wait(pe, s_xn2t, s.seq(4) + 1)
                    for j in range(2):
                        mm = pe.matmul(m0[:, j * N:(j + 1) * N], wqk_t[:, j, :], xn_t[:, :], start=True, stop=True)
                    mm.then_inc(s_qk, 1)
                if s.active(3):
                    b = s.seq(3)
                    pe.wait_ge(s_kvb, 2 * b + 2)
                    pe.wait_ge(s_expq, 2 * b + 2)
                    for t in range(NT):
                        pe.matmul(m1[:, t * NP * 2 * VW:(t + 1) * NP * 2 * VW], eps8[:, :],
                                  kvb[:, :, :].rearrange("p n c -> p (n c)"), start=(t == 0), stop=False,
                                  skip_group_check=True)
                    for t in range(NT):
                        for n in range(NP):
                            c = (t * NP + n) * 2 * VW
                            mm = pe.matmul(m1[:, c:c + 2 * VW], eq_t[:, n, t * P:(t + 1) * P], kvb[:, n, :],
                                           start=False, stop=True, skip_group_check=True)
                    mm.then_inc(s_out, 1)
                if s.active(2):
                    b = s.seq(2)
                    pe.wait_ge(s_maxq, 2 * b + 1)
                    features(s, u, 1, 1, s_ck)
                if s.active(4):
                    b = s.seq(4)
                    pe.wait_ge(s_xn2t, b + 1)
                    wait(pe, s_maxq, 2 * done(s.seq(2) + 1))
                    wait(pe, s_expq, 2 * done(s.seq(2)))
                    wait(pe, s_relu, b)
                    for c in range(FC):
                        mm = pe.matmul(z[:, c * N:(c + 1) * N], wfc_t[:, c, :], xn2_t[:, :],
                                       start=True, stop=True)
                    mm.then_inc(s_ff1, 1)
                if s.active(1):
                    b = s.seq(1)
                    pe.wait_ge(s_lo, 2 * b + 2)
                    for t in range(NT):
                        mm = pe.matmul(m0[:, t * D:(t + 1) * D], xn_t[:, t * P:(t + 1) * P], wv_t[:, :],
                                       start=True, stop=True)
                    mm.then_inc(s_v, 1)
                if s.active(3):
                    b = s.seq(3)
                    pe.wait_ge(s_att, b + 1)
                    for t in range(NT):
                        mm = pe.transpose(m1[:, t * P:(t + 1) * P],
                                          att[:, t * H:(t + 1) * H, :].rearrange("p h d -> p (h d)"), ident)
                    mm.then_inc(s_attt, 1)
                if s.active(2):
                    b = s.seq(2)
                    pe.wait_ge(s_spq, 4 * b + 4)
                    wait(pe, s_vsb, done(s.seq(1) + 1))
                    wait(pe, s_xn2t, s.seq(4) + 1)
                    for t in range(NT):
                        mm = pe.transpose(m0[:, t * P // 2:(t + 1) * P // 2].bitcast(BF16), parts_q[:, t, :],
                                          ident_bf[:, :])
                    mm.then_inc(s_ptq, 1)
                if s.active(3):
                    b = s.seq(3)
                    pe.wait_ge(s_attt_sb, b + 1)
                    for t in range(NT):
                        mm = pe.matmul(m1[:, t * D:(t + 1) * D], att_t[:, t * P:(t + 1) * P], wp_t[:, :],
                                       start=True, stop=True)
                    mm.then_inc(s_proj, 1)
                if s.active(2):
                    b = s.seq(2)
                    pe.wait_ge(s_ptq_sb, b + 1)
                    wait(pe, s_relu, s.seq(4) + 1)
                    features_t(s, 0)
                    sub_max_k(s, v, 0)
                    pe.wait_ge(s_expq, 2 * b + 1)
                    features_t(s, 1)
                if s.active(4):
                    b = s.seq(4)
                    pe.wait_ge(s_hsq, 2 * b + 2)
                    wait(pe, s_ptq_sb, done(s.seq(2) + 1))
                    for t in range(NT):
                        for c in range(FC):
                            mm = pe.matmul(m0[:, t * D:(t + 1) * D], hsq[:, c, t * P:(t + 1) * P],
                                           wpr_t[:, c, :], start=(c == 0), stop=(c == FC - 1))
                    mm.then_inc(s_y, 1)
                if s.active(2):
                    sub_max_k(s, u, 1)

            def sub_max_k(s, w, t):
                b = s.seq(2)
                pe.wait_ge(s_spk, 8 * b + 4 * t + 4)
                if t == 0:
                    wait(pe, s_a, s.seq(3) + 1)
                else:
                    pe.wait_ge(s_ptk_sb, 2 * b + 1)
                pe.transpose(m1[:, 0:P // 2].bitcast(BF16), parts_k[:, t, :], ident_bf[:, :]).then_inc(s_ptk, 1)
                pe.wait_ge(s_ptk_sb, 2 * b + t + 1)
                for c in range(2):
                    mm = pe.matmul(w[:, c * 512:(c + 1) * 512], parts_kt[:, t * P:(t + 1) * P],
                                   ind[:, c * 512:(c + 1) * 512], start=False, stop=True, skip_group_check=True)
                mm.then_inc(s_ksub, 1)

            slots(pe, body)

        @block.vector
        def _(dve):
            dve.wait_ge(s_const, 16 * N_CONST)
            dve.tensor_copy(pm16[:, :, :], pm_raw[:, :].unsqueeze(1).broadcast_to([M, 4 * HG, HD])).then_inc(s_pmrep, 1)
            dve.wait_ge(s_wtr, 4)
            for j in range(HG):
                op = dve.tensor_scalar(pf[:, j, :], m1[:, 0:M], head_mask[:, j:j + 1], SPLIT_SCALE, ALU.mult,
                                       ALU.mult)
                op.then_inc(s_pmrep, 1)
            dve.wait_ge(s_pmrep, 1 + HG)
            dve.tensor_copy(pf_hi[:, :, :], pf[:, :, :]).then_inc(s_pmrep, 1)
            dve.wait_ge(s_pmrep, 2 + HG)
            dve.tensor_tensor(pf_lo[:, :, :], pf[:, :, :], pf_hi[:, :, :], ALU.subtract).then_inc(s_pmrep, 1)
            dve.tensor_scalar(pst_a[:, :], pf_hi[:, :, :].rearrange("p h m -> p (h m)"), cst[:, P + HG:P + HG + 1],
                              None, ALU.mult).then_inc(s_pmrep, 1)
            dve.wait_ge(s_pmrep, 4 + HG)
            dve.scalar_tensor_tensor(pst[:, :], pf_lo[:, :, :].rearrange("p h m -> p (h m)"),
                                     cst[:, P + HG + 1:P + HG + 2], pst_a[:, :], ALU.mult, ALU.add).then_inc(s_prep, 1)

            def stats(k, b, tiles, ready):
                for sm, value in ready:
                    wait(dve, sm, value)
                for t in range(NT):
                    dve.bn_stats(st[k][:, t, :], tiles[t]).then_inc(s_stat[k], 1)
                wait(dve, s_rstd[k], b)
                for t in range(NT):
                    dve.wait_ge(s_stat[k], 2 * b + t + 1)
                    settle(dve)
                    dve.bn_aggr(mv[k][:, t, :], st[k][:, t, :]).then_inc(s_mv[k], 1)

            def maxima(w, nm, t, s_done):
                dve.tensor_reduce(nm[:, t, :], w[:, :].rearrange("p (h m) -> p h m", h=H), AX_X, ALU.max,
                                  negate=True).then_inc(s_done, 1)

            def body(s):
                u, v, z = wide[s.off % 2], wide[1 - s.off % 2], wide[2]
                if s.active(2):
                    b = s.seq(2)
                    wait(dve, s_spq, 4 * b)
                    dve.wait_ge(s_cq, 2 * b + 1)
                    maxima(u, nmax_q, 0, s_maxq)
                    dve.wait_ge(s_cq, 2 * b + 2)
                    maxima(z, nmax_q, 1, s_maxq)
                if s.active(1):
                    b = s.seq(1)
                    dve.wait_ge(s_hi, 2 * b + 2)
                    for j in range(2):
                        dve.scalar_tensor_tensor(lo[:, j, :], m0[:, j * N:(j + 1) * N], bq[:, j:j + 1],
                                                 hi[:, j, :], ALU.add, ALU.subtract).then_inc(s_lo, 1)
                if s.active(0):
                    b, p = s.seq(0), s.par(0)
                    stats(0, b, [xin[p][:, t, :] for t in range(NT)], [(s_xin[p], 16 * (s.round(0) + 1))])
                if s.active(2):
                    b = s.seq(2)
                    wait(dve, s_spk, 8 * b)
                    dve.wait_ge(s_ck, 2 * b + 1)
                    maxima(v, nmax_k, 0, s_maxk)
                if s.active(3):
                    b = s.seq(3)
                    dve.wait_ge(s_out, b + 1)
                    o = m1[:, 0:NT * H * VW].rearrange("p (h c) -> p h c", c=VW)
                    dve.tensor_scalar(den[:, :], o[:, :, HD], 64.0 * EPS_FAVOR, None, ALU.add).then_inc(s_den, 1)
                    dve.wait_ge(s_den, b + 1)
                    dve.reciprocal(rden[:, :], den[:, :]).then_inc(s_rden, 1)
                    dve.wait_ge(s_rden, b + 1)
                    wait(dve, s_attt, b)
                    dve.tensor_tensor(att[:, :, :], o[:, :, 0:HD],
                                      rden[:, :].unsqueeze(2).broadcast_to([P, NT * H, HD]),
                                      ALU.mult).then_inc(s_att, 1)
                if s.active(2):
                    b = s.seq(2)
                    dve.wait_ge(s_ck, 2 * b + 2)
                    maxima(u, nmax_k, 1, s_maxk)
                if s.active(1):
                    b, p = s.seq(1), s.par(1)
                    dve.wait_ge(s_v, b + 1)
                    wait(dve, s_kv, b - 1)
                    dve.tensor_tensor(vaug[p][:, :, :, 0:HD],
                                      m0[:, 0:NT * D].rearrange("p (t h d) -> p t h d", t=NT, h=H),
                                      bv[:, :, :].rearrange("p t (h d) -> p t h d", h=H), ALU.add).then_inc(s_vsb, 1)
                if s.active(3):
                    b, p = s.seq(3), s.par(3)
                    dve.wait_ge(s_proj, b + 1)
                    wait(dve, s_x1n, 2 * b)
                    dve.tensor_tensor(a_sb[:, :, :], m1[:, 0:NT * D].rearrange("p (t d) -> p t d", t=NT),
                                      bp[:, :, :], ALU.add).then_inc(s_a, 1)
                    stats(1, b, [a_sb[:, t, :] for t in range(NT)], [(s_a, b + 1)])
                if s.active(4):
                    b = s.seq(4)
                    dve.wait_ge(s_y, b + 1)
                    wait(dve, s_cn, 2 * b)
                    y = m0[:, 0:NT * D]
                    dve.tensor_scalar(cnt[0][:, :], y, thresholds[0], None, ALU.is_gt).then_inc(s_cnt, 1)
                    for n in range(1, NUM_STEPS):
                        dve.wait_ge(s_cnt, NUM_STEPS * b + n)
                        dve.scalar_tensor_tensor(cnt[n % 2][:, :], y, thresholds[n], cnt[1 - n % 2][:, :],
                                                 ALU.is_gt, ALU.add).then_inc(s_cnt, 1)
                    stats(3, b, [cnt[0][:, t * D:(t + 1) * D] for t in range(NT)], [(s_cnt, NUM_STEPS * (b + 1))])
                if s.active(3):
                    b, p = s.seq(3), s.par(3)
                    stats(2, b, [x1[p][:, t, :] for t in range(NT)], [(s_x1, b + 1)])

            slots(dve, body)


_INS = ['L0_attn_x', 'L0_attn_qkv_w', 'L0_attn_qkv_b', 'L0_attn_proj_w', 'L0_attn_proj_b',
        'L0_attn_projection_matrix', 'L0_ffn_W_fc', 'L0_ffn_W_proj']


def kernel(**inputs):
    import numpy as _np
    import concourse.bacc as _bacc
    from concourse import mybir as _mybir
    from concourse.bass_utils import run_bass_kernel_spmd as _run

    rows = _np.arange(128)
    const = _np.zeros((128, 128 + 4 + 2), _np.float32)
    const[rows, rows] = 1
    const[rows, 128 + rows % 32 // 8] = 1
    const[rows, 132 + rows // 32 % 2] = 1
    indicator = _np.zeros((128, 16, 64), _np.float16)
    for part in range(3):
        indicator[16 * part + _np.arange(16), _np.arange(16)] = 1

    nc = _bacc.Bacc("TRN2", target_bir_lowering=False, num_devices=1)
    arrays, args = {}, []
    named = {**{name: inputs[name] for name in _INS}, "const": const, "indicator": indicator.reshape(128, 1024)}
    for name, value in named.items():
        a = _np.ascontiguousarray(value)
        arrays[f"in_{name}_dram"] = a
        args.append(nc.dram_tensor(f"in_{name}_dram", a.shape, _mybir.dt.from_np(a.dtype), kind="ExternalInput").ap())
    shape = inputs["L0_attn_x"].shape
    args.append(nc.dram_tensor("out_0_dram", shape, _mybir.dt.float32, kind="ExternalOutput").ap())
    sandwich_kernel(nc, *args)
    r = _run(nc, [arrays], core_ids=[0])
    return r.results[0]["out_0_dram"]
```

```python
from contextlib import ExitStack

import concourse.bass as bass
from concourse import mybir

F32 = mybir.dt.float32
F16 = mybir.dt.float16
BF16 = mybir.dt.bfloat16
ALU = mybir.AluOpType
ACT = mybir.ActivationFunctionType
AX_X = mybir.AxisListType.X

P = 128
EPS_LN = 1e-5
EPS_FAVOR = 1e-6
BETA = 0.9
NUM_STEPS = 5
SPLIT_SCALE = 64.0


def spike_thresholds():
    def spikes(y):
        m, n = 0.0, 0
        for _ in range(NUM_STEPS):
            m = BETA * m + y - (1.0 if m > 1.0 else 0.0)
            n += m > 1.0
        return n

    edges = []
    for n in range(1, NUM_STEPS + 1):
        low, high = 0.0, 4.0
        for _ in range(80):
            mid = (low + high) / 2
            low, high = (low, mid) if spikes(mid) >= n else (mid, high)
        edges.append(high)
    return edges


def sandwich_kernel(nc, x, qkv_w, qkv_b, proj_w, proj_b, pm, w_fc, w_proj, const, indicator, out):
    NB, N, D = x.shape
    M, HD = pm.shape
    H = D // HD
    FF = w_fc.shape[0]
    NT = N // P
    NG = P // 32
    HG = H // NG
    GW = HG * M
    NP = H // 2
    VW = HD + 1
    PW = 32
    MW = 2 * M + 1
    NR = NP // 4
    FC = FF // P
    HM = H * M
    EXP_SCALE = 1.0 / (SPLIT_SCALE * SPLIT_SCALE * float(HD) ** 0.5)
    EPS8 = 8.0 * EPS_FAVOR
    assert NT == 2 and HM == 1024 and FF == 512 and M == 64 and NB % 2 == 0
    thresholds = spike_thresholds()

    x_v = x.rearrange("b (t p) d -> b p t d", p=P)
    out_v = out.rearrange("b (t p) d -> b p t d", p=P)

    with ExitStack() as ctx:
        def sb(name, shape, dt=F32):
            return ctx.enter_context(nc.sbuf_tensor(name, shape, dt))

        def sem(name):
            return ctx.enter_context(nc.semaphore(name))

        cst = sb("cst", [P, P + HG + 2 + P])
        ident = cst[:, 0:P]
        head_mask = cst[:, P:P + HG]
        kv_mask = cst[:, P + HG + 2:]
        ident_bf = sb("ident_bf", [P, P], BF16)
        ind = sb("ind", [P, HM], F16)
        neg_half = sb("neg_half", [P, NT])
        w_raw = sb("w_raw", [P, 3 + 1 + FC + FC, P])
        pm16 = sb("pm16", [M, 4 * HG, HD])
        pm_raw = sb("pm_raw", [M, HD])
        bq_raw = sb("bq_raw", [P, 2])
        bq = sb("bq", [P, 2])
        bv = sb("bv", [P, NT, D])
        bp = sb("bp", [P, NT, D])
        wqk_t = sb("wqk_t", [P, 2, D])
        wv_t = sb("wv_t", [P, D])
        wp_t = sb("wp_t", [P, D])
        wfc_t = sb("wfc_t", [P, FC, P])
        wpr_t = sb("wpr_t", [P, FC, D])
        pf = sb("pf", [P, HG, M])
        pf_hi = sb("pf_hi", [P, HG, M], F16)
        pf_lo = sb("pf_lo", [P, HG, M], F16)
        pst_a = sb("pst_a", [P, HG * M], F16)
        pst = sb("pst", [P, HG * M], F16)

        xin = [sb(f"xin{i}", [P, NT, D]) for i in range(2)]
        xres = sb("xres", [P, NT, D])
        xn = sb("xn", [P, NT, D])
        xn_t = sb("xn_t", [P, N])
        hi = sb("hi", [P, 2, N], F16)
        lo = sb("lo", [P, 2, N], F16)
        stack = [sb(f"stack{i}", [P, NG, 2, N], F16) for i in range(2)]
        vaug = [sb(f"vaug{i}", [P, NT, NP, PW]) for i in range(2)]
        nmax_q = sb("nmax_q", [P, NT, H])
        nmax_k = sb("nmax_k", [P, NT, H])
        rem_q = sb("rem_q", [P, NT, H])
        rem_k = sb("rem_k", [P, NT, H])
        parts_q = sb("parts_q", [P, NT, P], BF16)
        parts_k = sb("parts_k", [P, NT, P], BF16)
        parts_qt = sb("parts_qt", [P, N], BF16)
        parts_kt = sb("parts_kt", [P, N], BF16)
        ek = sb("ek", [P, NT, NP, MW])
        eq_t = sb("eq_t", [P, NP, N])
        kvt = sb("kvt", [P, NR, P])
        kv_sum = sb("kv_sum", [P, NR])
        kv_sum8 = sb("kv_sum8", [P, NR])
        kvb = sb("kvb", [P, NP, PW])
        out_t = sb("out_t", [P, NR, N])
        den = sb("den", [P, NT * H])
        rden = sb("rden", [P, NT * H])
        att = sb("att", [P, NT * H, HD])
        att_t = sb("att_t", [P, N])
        a_sb = sb("a_sb", [P, NT, D])
        x1 = [sb(f"x1_{i}", [P, NT, D]) for i in range(2)]
        x1n = sb("x1n", [P, NT, D])
        xn2 = sb("xn2", [P, NT, D])
        xn2_t = sb("xn2_t", [P, N])
        y_sb = sb("y_sb", [P, NT * D])
        relu = sb("relu", [P, FC, N])
        hsq = sb("hsq", [P, FC, N])
        cnt = [sb(f"cnt{i}", [P, NT * D]) for i in range(2)]
        cn = sb("cn", [P, NT, D])
        xo = sb("xo", [P, NT, D])
        st = [sb(f"st{k}", [P, NT, 6]) for k in range(4)]
        mv = [sb(f"mv{k}", [P, NT, 2]) for k in range(4)]
        var = [sb(f"var{k}", [P, NT]) for k in range(4)]
        nmean = [sb(f"nmean{k}", [P, NT]) for k in range(4)]
        rstd = [sb(f"rstd{k}", [P, NT]) for k in range(4)]

        wide = [ctx.enter_context(nc.psum_tensor(f"wide{i}", [P, HM], F32)) for i in range(3)]
        m0 = ctx.enter_context(nc.psum_tensor("m0", [P, 512], F32))
        m1 = ctx.enter_context(nc.psum_tensor("m1", [P, 512], F32))

        s_settled = [sem("s_settled_dve"), sem("s_settled_pool")]
        s_const = sem("s_const")
        s_zero = sem("s_zero")
        s_wtr = sem("s_wtr")
        s_wcopy = sem("s_wcopy")
        s_prep = sem("s_prep")
        s_idbf = sem("s_idbf")
        s_pmrep = sem("s_pmrep")
        s_xin = [sem("s_xin0"), sem("s_xin1")]
        s_xres = sem("s_xres")
        s_stat = [sem(f"s_stat{k}") for k in range(4)]
        s_mv = [sem(f"s_mv{k}") for k in range(4)]
        s_var = [sem(f"s_var{k}") for k in range(4)]
        s_rstd = [sem(f"s_rstd{k}") for k in range(4)]
        s_xn = sem("s_xn")
        s_xt = sem("s_xt")
        s_xnt = sem("s_xnt")
        s_qk = sem("s_qk")
        s_hi = sem("s_hi")
        s_lo = sem("s_lo")
        s_stack = [sem("s_stack0"), sem("s_stack1")]
        s_v = sem("s_v")
        s_vsb = sem("s_vsb")
        s_cq = sem("s_cq")
        s_ck = sem("s_ck")
        s_maxq = sem("s_maxq")
        s_maxk = sem("s_maxk")
        s_spq = sem("s_spq")
        s_spk = sem("s_spk")
        s_ptq = sem("s_ptq")
        s_ptk = sem("s_ptk")
        s_ptq_sb = sem("s_ptq_sb")
        s_ptk_sb = sem("s_ptk_sb")
        s_qt = sem("s_qt")
        s_ksub = sem("s_ksub")
        s_expq = sem("s_expq")
        s_expk = sem("s_expk")
        s_kv = sem("s_kv")
        s_kvt = sem("s_kvt")
        s_kvsum = sem("s_kvsum")
        s_trkv = sem("s_trkv")
        s_kvb = sem("s_kvb")
        s_outt = sem("s_outt")
        s_out = sem("s_out")
        s_trout = sem("s_trout")
        s_den = sem("s_den")
        s_rden = sem("s_rden")
        s_att = sem("s_att")
        s_attt = sem("s_attt")
        s_attt_sb = sem("s_attt_sb")
        s_proj = sem("s_proj")
        s_a = sem("s_a")
        s_x1n = sem("s_x1n")
        s_x1 = sem("s_x1")
        s_xn2 = sem("s_xn2")
        s_x2t = sem("s_x2t")
        s_xn2t = sem("s_xn2t")
        s_ff1 = sem("s_ff1")
        s_relu = sem("s_relu")
        s_hsq = sem("s_hsq")
        s_y = sem("s_y")
        s_ysb = sem("s_ysb")
        s_cnt = sem("s_cnt")
        s_cn = sem("s_cn")
        s_xo = sem("s_xo")
        s_store = sem("s_store")

        def wait(eng, s, value):
            if not isinstance(value, int) or value > 0:
                eng.wait_ge(s, value)

        def settle(eng):
            eng.sem_inc(s_settled[eng is nc.gpsimd], 1)

        class Slot:

            def __init__(self, half, off):
                self.half, self.base, self.off = half, half * 2, off

            def seq(self, k):
                return self.base + (self.off - k)

            def par(self, k):
                return (self.off - k) % 2

            def round(self, k):
                return self.half + (self.off - k - self.par(k)) // 2

            def active(self, k):
                return not isinstance(self.base, int) or 0 <= self.seq(k) < NB

        STAGES = 6
        PEELED = 6
        LAST = NB + STAGES - 1

        def slots(eng, body):
            for t in range(PEELED):
                body(Slot(t // 2, t % 2))
            with eng.Fori(PEELED // 2, NB // 2) as i:
                for off in range(2):
                    body(Slot(i, off))
            for t in range(NB, LAST):
                body(Slot(t // 2, t % 2))

        def done(value):
            return min(value, NB) if isinstance(value, int) else value

        block = ctx.enter_context(nc.Block())

        N_CONST = 12
        ZEROED = 10

        @block.sync
        def _(sp):
            sp.dma_start(cst[:, :], const).then_inc(s_const, 16)
            sp.dma_start(w_raw[:, 0:3, :], qkv_w.rearrange("(c p) d -> p c d", p=P)).then_inc(s_const, 16)
            sp.dma_start(pm_raw[:, :], pm).then_inc(s_const, 16)
            sp.dma_start(w_raw[:, 3, :], proj_w).then_inc(s_const, 16)
            sp.dma_start(w_raw[:, 4:4 + FC, :], w_fc.rearrange("(c p) d -> p c d", p=P)).then_inc(s_const, 16)
            sp.dma_start(w_raw[:, 4 + FC:, :], w_proj.rearrange("d (c f) -> d c f", c=FC)).then_inc(s_const, 16)
            with nc.allow_non_contiguous_dma(reason="two short bias columns"):
                sp.dma_start(bq_raw[:, :], qkv_b[0:2 * D].rearrange("(c p) -> p c", p=P)).then_inc(s_const, 16)
            sp.dma_start(ind[:, :], indicator).then_inc(s_const, 16)
            for t in range(NT):
                sp.dma_start(bv[:, t, :], qkv_b[2 * D:3 * D].rearrange("(a d) -> a d", a=1).broadcast_to([P, D])).then_inc(s_const, 16)
                sp.dma_start(bp[:, t, :], proj_b.rearrange("(a d) -> a d", a=1).broadcast_to([P, D])).then_inc(s_const, 16)

            def body(s):
                if s.active(0):
                    b, p = s.seq(0), s.par(0)
                    wait(sp, s_xn, 2 * (b - 1))
                    sp.dma_start(xin[p][:, :, :], x_v[b]).then_inc(s_xin[p], 16)
                if s.active(3):
                    b = s.seq(3)
                    wait(sp, s_x1, b)
                    sp.dma_start(xres[:, :, :], x_v[b]).then_inc(s_xres, 16)
                if s.active(1):
                    b, p = s.seq(1), s.par(1)
                    wait(sp, s_hi, 2 * b + 2)
                    wait(sp, s_qt, 2 * (b - 1))
                    wait(sp, s_ck, 2 * (b - 1))
                    for g in range(NG):
                        for r in range(2):
                            sp.dma_start(stack[p][32 * r:32 * r + 32, g, :, :],
                                         hi[32 * g:32 * g + 32, :, :]).then_inc(s_stack[p], 16)
                    wait(sp, s_lo, 2 * b + 2)
                    for g in range(NG):
                        for r in range(2, 4):
                            sp.dma_start(stack[p][32 * r:32 * r + 32, g, :, :],
                                         lo[32 * g:32 * g + 32, :, :]).then_inc(s_stack[p], 16)

            slots(sp, body)

        @block.gpsimd
        def _(pool):
            pool.memset(parts_q[:, :, :], 0.0).then_inc(s_zero, 1)
            pool.memset(parts_k[:, :, :], 0.0).then_inc(s_zero, 1)
            for i in range(2):
                pool.memset(vaug[i][:, :, :, :], 0.0).then_inc(s_zero, 1)
            pool.memset(ek[:, :, :, 2 * M:MW], EPS8).then_inc(s_zero, 1)
            pool.memset(neg_half[:, :], -0.5).then_inc(s_zero, 1)
            pool.wait_ge(s_zero, 6)
            for i in range(2):
                for h in range(2):
                    c = h * VW + HD
                    pool.memset(vaug[i][:, :, :, c:c + 1], 1.0).then_inc(s_zero, 1)
            pool.wait_ge(s_zero, ZEROED)

            def inv_std(k, b, eps, last_readers):
                own = 2 if k in (1, 3) else 1
                for sm, value in last_readers:
                    wait(pool, sm, value)
                pool.wait_ge(s_mv[k], 2 * b + 2)
                settle(pool)
                pool.tensor_scalar(var[k][:, :], mv[k][:, :, 1], eps, None, ALU.add).then_inc(s_var[k], 1)
                if own == 2:
                    pool.tensor_scalar(nmean[k][:, :], mv[k][:, :, 0], -1.0, None, ALU.mult).then_inc(s_var[k], 1)
                pool.wait_ge(s_var[k], own * (b + 1))
                pool.tensor_tensor(rstd[k][:, :], var[k][:, :], neg_half[:, :], ALU.pow).then_inc(s_rstd[k], 1)

            def normalize(k, t, dst, src, done_sem):
                settle(pool)
                pool.tensor_scalar(dst, src, nmean[k][:, t:t + 1], rstd[k][:, t:t + 1], ALU.add,
                                   ALU.mult).then_inc(done_sem, 1)

            def split(nm, rem, parts, lo_t, hi_t, s_split, first):
                n = nm[:, lo_t:hi_t, :]
                r = rem[:, lo_t:hi_t, :]
                a = [parts[:, lo_t:hi_t, H * i:H * (i + 1)] for i in range(3)]
                settle(pool)
                pool.tensor_copy(a[0], n).then_inc(s_split, 1)
                pool.wait_ge(s_split, first + 1)
                pool.tensor_tensor(r, n, a[0], ALU.subtract).then_inc(s_split, 1)
                pool.wait_ge(s_split, first + 2)
                settle(pool)
                pool.tensor_copy(a[1], r).then_inc(s_split, 1)
                pool.wait_ge(s_split, first + 3)
                pool.tensor_tensor(a[2], r, a[1], ALU.subtract).then_inc(s_split, 1)

            def body(s):
                if s.active(4):
                    b = s.seq(4)
                    inv_std(2, b, EPS_LN, [(s_xn2, 2 * b)])
                if s.active(2):
                    b = s.seq(2)
                    pool.wait_ge(s_maxq, 2 * b + 2)
                    wait(pool, s_ptq, b)
                    split(nmax_q, rem_q, parts_q, 0, NT, s_spq, 4 * b)
                    split_k(b, 0)
                if s.active(0):
                    b = s.seq(0)
                    inv_std(0, b, EPS_LN, [(s_xn, 2 * b)])
                if s.active(2):
                    split_k(s.seq(2), 1)
                if s.active(5):
                    b, p = s.seq(5), s.par(5)
                    inv_std(3, b, EPS_LN * NUM_STEPS * NUM_STEPS, [])
                    pool.wait_ge(s_rstd[3], b + 1)
                    for t in range(NT):
                        normalize(3, t, cn[:, t, :], cnt[0][:, t * D:(t + 1) * D], s_cn)
                    pool.wait_ge(s_cn, 2 * b + 2)
                    wait(pool, s_store, 16 * b)
                    pool.tensor_tensor(xo[:, :, :], cn[:, :, :], x1[p][:, :, :], ALU.add).then_inc(s_xo, 1)
                if s.active(3):
                    b, p = s.seq(3), s.par(3)
                    inv_std(1, b, EPS_LN, [])
                    pool.wait_ge(s_rstd[1], b + 1)
                    for t in range(NT):
                        normalize(1, t, x1n[:, t, :], a_sb[:, t, :], s_x1n)
                    pool.wait_ge(s_x1n, 2 * b + 2)
                    pool.wait_ge(s_xres, 16 * (b + 1))
                    wait(pool, s_xo, b - 1)
                    pool.tensor_tensor(x1[p][:, :, :], x1n[:, :, :], xres[:, :, :], ALU.add).then_inc(s_x1, 1)
                if s.active(5):
                    b = s.seq(5)
                    pool.wait_ge(s_xo, b + 1)
                    pool.dma_start(out_v[b], xo[:, :, :]).then_inc(s_store, 16)

            def split_k(b, t):
                pool.wait_ge(s_maxk, 2 * b + t + 1)
                if t == 0:
                    wait(pool, s_ptk, 2 * b)
                split(nmax_k, rem_k, parts_k, t, t + 1, s_spk, 8 * b + 4 * t)

            slots(pool, body)
            pool.wait_ge(s_store, 16 * NB)

        @block.scalar
        def _(act):
            act.wait_ge(s_const, 16 * N_CONST)
            act.activation(ident_bf[:, :], ident, ACT.Copy).then_inc(s_idbf, 1)
            act.activation(bq[:, :], bq_raw[:, :], ACT.Copy, scale=SPLIT_SCALE).then_inc(s_idbf, 1)
            act.wait_ge(s_wtr, 1)
            act.activation(wqk_t[:, :, :], wide[0][:, 0:2 * P].rearrange("p (c d) -> p c d", c=2), ACT.Copy,
                           scale=SPLIT_SCALE).then_inc(s_wcopy, 1)
            act.activation(wv_t[:, :], wide[0][:, 2 * P:3 * P], ACT.Copy).then_inc(s_wcopy, 1)
            act.activation(wp_t[:, :], wide[0][:, 3 * P:4 * P], ACT.Copy).then_inc(s_wcopy, 1)
            act.wait_ge(s_wtr, 2)
            act.activation(wfc_t[:, :, :], wide[1][:, 0:FC * P].rearrange("p (c d) -> p c d", c=FC),
                           ACT.Copy).then_inc(s_wcopy, 1)
            act.wait_ge(s_wtr, 3)
            act.activation(wpr_t[:, :, :], wide[2][:, 0:FC * P].rearrange("p (c d) -> p c d", c=FC),
                           ACT.Copy).then_inc(s_wcopy, 1)

            def body(s):
                if s.active(1):
                    b, p = s.seq(1), s.par(1)
                    act.wait_ge(s_xt, b + 1)
                    wait(act, s_v, b)
                    act.activation(xn_t[:, :], m0[:, 0:N], ACT.Copy).then_inc(s_xnt, 1)
                if s.active(3):
                    exp_k(s, 3, 1)
                if s.active(1):
                    b, p = s.seq(1), s.par(1)
                    act.wait_ge(s_qk, b + 1)
                    wait(act, s_stack[1 - p], 16 * 4 * NG * (s.round(1) + p))
                    for j in range(2):
                        act.activation(hi[:, j, :], m0[:, j * N:(j + 1) * N], ACT.Identity,
                                       bias=bq[:, j:j + 1]).then_inc(s_hi, 1)
                if s.active(3):
                    b = s.seq(3)
                    act.wait_ge(s_trkv, b + 1)
                    wait(act, s_out, b)
                    act.activation(kvb[:, :, :], m1[:, 0:NP * PW].rearrange("p (n c) -> p n c", n=NP),
                                   ACT.Copy).then_inc(s_kvb, 1)
                if s.active(4):
                    b = s.seq(4)
                    act.wait_ge(s_x2t, b + 1)
                    wait(act, s_ff1, b)
                    act.activation(xn2_t[:, :], m0[:, 0:N], ACT.Copy).then_inc(s_xn2t, 1)
                if s.active(3):
                    b = s.seq(3)
                    act.wait_ge(s_out, b + 1)
                    wait(act, s_trout, b)
                    act.wait_ge(s_kvsum, b + 1)
                    for r in range(NR):
                        act.activation(out_t[:, r, :], m1[:, r * N:(r + 1) * N], ACT.Identity,
                                       bias=kv_sum8[:, r:r + 1]).then_inc(s_outt, 1)
                if s.active(4):
                    b = s.seq(4)
                    act.wait_ge(s_ff1, b + 1)
                    act.activation(relu[:, :, :], wide[2][:, :].rearrange("p (c n) -> p c n", c=FC),
                                   ACT.Relu).then_inc(s_relu, 1)
                if s.active(2):
                    b = s.seq(2)
                    act.wait_ge(s_ptq, b + 1)
                    wait(act, s_qt, 2 * b)
                    act.activation(parts_qt[:, :], m0[:, 0:N // 2].bitcast(BF16), ACT.Copy).then_inc(s_ptq_sb, 1)
                if s.active(3):
                    b = s.seq(3)
                    act.wait_ge(s_attt, b + 1)
                    wait(act, s_proj, b)
                    act.activation(att_t[:, :], m1[:, 0:N], ACT.Copy).then_inc(s_attt_sb, 1)
                if s.active(2):
                    copy_parts_k(s, 0)
                if s.active(4):
                    b = s.seq(4)
                    act.wait_ge(s_relu, b + 1)
                    wait(act, s_y, b)
                    act.activation(hsq[:, :, :], relu[:, :, :], ACT.Square).then_inc(s_hsq, 1)
                if s.active(2):
                    exp_q(s, 0)
                    copy_parts_k(s, 1)
                    exp_k(s, 2, 0)
                if s.active(4):
                    b = s.seq(4)
                    act.wait_ge(s_y, b + 1)
                    wait(act, s_cnt, NUM_STEPS * b)
                    act.activation(y_sb[:, :], m0[:, 0:NT * D], ACT.Copy).then_inc(s_ysb, 1)
                if s.active(2):
                    exp_q(s, 1)

            def copy_parts_k(s, t):
                b = s.seq(2)
                act.wait_ge(s_ptk, 2 * b + t + 1)
                wait(act, s_ksub, 2 * b + t - 1)
                act.activation(parts_kt[:, t * P:(t + 1) * P], m0[:, 0:P // 2].bitcast(BF16),
                               ACT.Copy).then_inc(s_ptk_sb, 1)

            def exp_q(s, j):
                b = s.seq(2)
                act.wait_ge(s_qt, 2 * b + j + 1)
                if j == 0:
                    wait(act, s_out, b)
                act.activation(eq_t[:, 4 * j:4 * j + 4, :], wide[2][:, :].rearrange("p (c n) -> p c n", c=4),
                               ACT.Exp, scale=EXP_SCALE).then_inc(s_expq, 1)

            def exp_k(s, stage, t):
                b = s.seq(stage)
                w = wide[1 - s.off % 2]
                act.wait_ge(s_ksub, 2 * b + t + 1)
                wait(act, s_kv, b)
                act.activation(ek[:, t, :, 0:2 * M], w[:, :].rearrange("p (n c) -> p n c", n=NP), ACT.Exp,
                               scale=EXP_SCALE).then_inc(s_expk, 1)

            slots(act, body)

        @block.tensor
        def _(pe):
            pe.wait_ge(s_const, 16 * N_CONST)
            for c in range(4):
                mm = pe.transpose(wide[0][:, c * P:(c + 1) * P], w_raw[:, c, :], ident)
            mm.then_inc(s_wtr, 1)
            for c in range(FC):
                mm = pe.transpose(wide[1][:, c * P:(c + 1) * P], w_raw[:, 4 + c, :], ident)
            mm.then_inc(s_wtr, 1)
            for c in range(FC):
                mm = pe.transpose(wide[2][:, c * P:(c + 1) * P], w_raw[:, 4 + FC + c, :], ident)
            mm.then_inc(s_wtr, 1)
            pe.wait_ge(s_pmrep, 1)
            pe.matmul(m1[:, 0:M], pm16[:, :, :].rearrange("m r d -> m (r d)"), cst[0:M, 0:M], start=True,
                      stop=True).then_inc(s_wtr, 1)
            pe.wait_ge(s_wcopy, 5)
            pe.wait_ge(s_prep, 1)
            pe.wait_ge(s_idbf, 2)
            pe.wait_ge(s_zero, ZEROED)

            def features(s, w, j, t, done_sem):
                p = s.par(2)
                for g in range(NG):
                    mm = pe.matmul(w[:, g * GW:(g + 1) * GW], stack[p][:, g, j, t * P:(t + 1) * P], pst[:, :],
                                   start=(g % 2 == 0), stop=False, skip_group_check=True)
                mm.then_inc(done_sem, 1)

            def features_t(s, half):
                p = s.par(2)
                for i in range(NP // 2):
                    pair = half * (NP // 2) + i
                    g, e = pair // 2, pair % 2
                    o = wide[2][:, i * N:(i + 1) * N]
                    pe.matmul(o, pst[:, e * P:(e + 1) * P], stack[p][:, g, 0, :],
                              start=(i % 2 == 0), stop=False, skip_group_check=True)
                    mm = pe.matmul(o, ind[:, pair * P:(pair + 1) * P], parts_qt[:, :], start=False,
                                   stop=True, skip_group_check=True)
                mm.then_inc(s_qt, 1)

            def body(s):
                u, v, z = wide[s.off % 2], wide[1 - s.off % 2], wide[2]
                b1, b2, b3, b4 = (s.seq(k) for k in range(1, 5))
                if s.active(1):
                    pe.wait_ge(s_xn, 2 * b1 + 2)
                    wait(pe, s_ysb, b4)
                    wait(pe, s_ptk_sb, 2 * b2)
                    wait(pe, s_vsb, 2 * b1)
                    for t in range(NT):
                        mm = pe.transpose(m0[:, t * P:(t + 1) * P], xn[:, t, :], ident)
                    mm.then_inc(s_xt, 1)
                if s.active(2):
                    pe.wait_ge(s_stack[s.par(2)], 16 * 4 * NG * (s.round(2) + 1))
                    wait(pe, s_expk, 2 * b2 - 1)
                    features(s, u, 0, 0, s_cq)
                if s.active(2):
                    wait(pe, s_expq, 2 * b2)
                    features(s, z, 0, 1, s_cq)
                if s.active(1):
                    pe.wait_ge(s_xnt, b1 + 1)
                    for j in range(2):
                        mm = pe.matmul(m0[:, j * N:(j + 1) * N], wqk_t[:, j, :], xn_t[:, :], start=True, stop=True)
                    mm.then_inc(s_qk, 1)
                if s.active(3):
                    p = s.par(3)
                    pe.wait_ge(s_vsb, 2 * b3 + 2)
                    wait(pe, s_a, b3)
                    for t in range(NT):
                        pe.wait_ge(s_expk, 2 * b3 + t + 1)
                        for n in range(NP):
                            c, r = n % 4, n // 4
                            mm = pe.matmul(m1[c * PW:(c + 1) * PW, r * MW:(r + 1) * MW], vaug[p][:, t, n, :],
                                           ek[:, t, n, :], start=(t == 0 and r == 0), stop=(t == NT - 1),
                                           tile_position=(0, c * PW), skip_group_check=True)
                    mm.then_inc(s_kv, 1)
                if s.active(2):
                    wait(pe, s_expk, 2 * b2)
                    features(s, v, 1, 0, s_ck)
                    pe.wait_ge(s_maxq, 2 * b2 + 1)
                    features(s, u, 1, 1, s_ck)
                if s.active(3):
                    pe.wait_ge(s_kvt, 2 * b3 + 2)
                    for r in range(NR):
                        mm = pe.transpose(m1[:, r * P:(r + 1) * P], kvt[:, r, :], ident)
                    mm.then_inc(s_trkv, 1)
                if s.active(4):
                    pe.wait_ge(s_xn2, 2 * b4 + 2)
                    wait(pe, s_lo, 2 * done(b1 + 1))
                    wait(pe, s_ysb, b4)
                    wait(pe, s_ptk_sb, 2 * done(b2))
                    for t in range(NT):
                        mm = pe.transpose(m0[:, t * P:(t + 1) * P], xn2[:, t, :], ident)
                    mm.then_inc(s_x2t, 1)
                if s.active(3):
                    pe.wait_ge(s_kvb, b3 + 1)
                    pe.wait_ge(s_expq, 2 * b3 + 2)
                    for n in range(NP):
                        c, r = n % 4, n // 4
                        mm = pe.matmul(m1[c * PW:(c + 1) * PW, r * N:(r + 1) * N], kvb[:, n, :], eq_t[:, n, :],
                                       start=(r == 0), stop=True, tile_position=(0, c * PW),
                                       skip_group_check=True)
                    mm.then_inc(s_out, 1)
                if s.active(1):
                    pe.wait_ge(s_lo, 2 * b1 + 2)
                    wait(pe, s_xn2t, b4 + 1)
                    for t in range(NT):
                        mm = pe.matmul(m0[:, t * D:(t + 1) * D], xn_t[:, t * P:(t + 1) * P], wv_t[:, :],
                                       start=True, stop=True)
                    mm.then_inc(s_v, 1)
                if s.active(3):
                    pe.wait_ge(s_outt, 2 * b3 + 2)
                    for t in range(NT):
                        for r in range(NR):
                            c = (t * NR + r) * P
                            mm = pe.transpose(m1[:, c:c + P], out_t[:, r, t * P:(t + 1) * P], ident)
                    mm.then_inc(s_trout, 1)
                if s.active(4):
                    pe.wait_ge(s_xn2t, b4 + 1)
                    wait(pe, s_maxq, 2 * done(b2 + 1))
                    wait(pe, s_expq, 2 * done(b2))
                    wait(pe, s_relu, b4)
                    for c in range(FC):
                        mm = pe.matmul(z[:, c * N:(c + 1) * N], wfc_t[:, c, :], xn2_t[:, :],
                                       start=True, stop=True)
                    mm.then_inc(s_ff1, 1)
                if s.active(2):
                    pe.wait_ge(s_spq, 4 * b2 + 4)
                    wait(pe, s_vsb, 2 * done(b1 + 1))
                    wait(pe, s_xn2t, b4 + 1)
                    for t in range(NT):
                        mm = pe.transpose(m0[:, t * P // 2:(t + 1) * P // 2].bitcast(BF16), parts_q[:, t, :],
                                          ident_bf[:, :])
                    mm.then_inc(s_ptq, 1)
                if s.active(3):
                    pe.wait_ge(s_att, b3 + 1)
                    for t in range(NT):
                        mm = pe.transpose(m1[:, t * P:(t + 1) * P],
                                          att[:, t * H:(t + 1) * H, :].rearrange("p h d -> p (h d)"), ident)
                    mm.then_inc(s_attt, 1)
                if s.active(2):
                    pe.wait_ge(s_ptq_sb, b2 + 1)
                    parts_k_t(s, 0)
                    wait(pe, s_relu, b4 + 1)
                    features_t(s, 0)
                if s.active(3):
                    pe.wait_ge(s_attt_sb, b3 + 1)
                    for t in range(NT):
                        mm = pe.matmul(m1[:, t * D:(t + 1) * D], att_t[:, t * P:(t + 1) * P], wp_t[:, :],
                                       start=True, stop=True)
                    mm.then_inc(s_proj, 1)
                if s.active(2):
                    sub_max_k(s, v, 0)
                    parts_k_t(s, 1)
                if s.active(4):
                    pe.wait_ge(s_hsq, b4 + 1)
                    wait(pe, s_ptk_sb, 2 * done(b2 + 1))
                    for t in range(NT):
                        for c in range(FC):
                            mm = pe.matmul(m0[:, t * D:(t + 1) * D], hsq[:, c, t * P:(t + 1) * P],
                                           wpr_t[:, c, :], start=(c == 0), stop=(c == FC - 1))
                    mm.then_inc(s_y, 1)
                if s.active(2):
                    pe.wait_ge(s_expq, 2 * b2 + 1)
                    features_t(s, 1)
                    sub_max_k(s, u, 1)

            def parts_k_t(s, t):
                b = s.seq(2)
                pe.wait_ge(s_spk, 8 * b + 4 * t + 4)
                wait(pe, s_ptk_sb, 2 * b + t)
                pe.transpose(m0[:, 0:P // 2].bitcast(BF16), parts_k[:, t, :], ident_bf[:, :]).then_inc(s_ptk, 1)

            def sub_max_k(s, w, t):
                b = s.seq(2)
                pe.wait_ge(s_ptk_sb, 2 * b + t + 1)
                for c in range(2):
                    mm = pe.matmul(w[:, c * 512:(c + 1) * 512], parts_kt[:, t * P:(t + 1) * P],
                                   ind[:, c * 512:(c + 1) * 512], start=False, stop=True, skip_group_check=True)
                mm.then_inc(s_ksub, 1)

            slots(pe, body)

        @block.vector
        def _(dve):
            dve.wait_ge(s_const, 16 * N_CONST)
            dve.tensor_copy(pm16[:, :, :], pm_raw[:, :].unsqueeze(1).broadcast_to([M, 4 * HG, HD])).then_inc(s_pmrep, 1)
            dve.wait_ge(s_wtr, 4)
            for j in range(HG):
                op = dve.tensor_scalar(pf[:, j, :], m1[:, 0:M], head_mask[:, j:j + 1], SPLIT_SCALE, ALU.mult,
                                       ALU.mult)
                op.then_inc(s_pmrep, 1)
            dve.wait_ge(s_pmrep, 1 + HG)
            dve.tensor_copy(pf_hi[:, :, :], pf[:, :, :]).then_inc(s_pmrep, 1)
            dve.wait_ge(s_pmrep, 2 + HG)
            dve.tensor_tensor(pf_lo[:, :, :], pf[:, :, :], pf_hi[:, :, :], ALU.subtract).then_inc(s_pmrep, 1)
            dve.tensor_scalar(pst_a[:, :], pf_hi[:, :, :].rearrange("p h m -> p (h m)"), cst[:, P + HG:P + HG + 1],
                              None, ALU.mult).then_inc(s_pmrep, 1)
            dve.wait_ge(s_pmrep, 4 + HG)
            dve.scalar_tensor_tensor(pst[:, :], pf_lo[:, :, :].rearrange("p h m -> p (h m)"),
                                     cst[:, P + HG + 1:P + HG + 2], pst_a[:, :], ALU.mult, ALU.add).then_inc(s_prep, 1)

            def stats(k, b, tiles, ready):
                for sm, value in ready:
                    wait(dve, sm, value)
                for t in range(NT):
                    dve.bn_stats(st[k][:, t, :], tiles[t]).then_inc(s_stat[k], 1)
                wait(dve, s_rstd[k], b)
                for t in range(NT):
                    dve.wait_ge(s_stat[k], 2 * b + t + 1)
                    settle(dve)
                    dve.bn_aggr(mv[k][:, t, :], st[k][:, t, :]).then_inc(s_mv[k], 1)

            def maxima(w, nm, t, s_done):
                dve.tensor_reduce(nm[:, t, :], w[:, :].rearrange("p (h m) -> p h m", h=H), AX_X, ALU.max,
                                  negate=True).then_inc(s_done, 1)

            def normalize(k, b, dst, src, s_done, last_reader):
                dve.wait_ge(s_rstd[k], b + 1)
                wait(dve, last_reader, b)
                for t in range(NT):
                    dve.tensor_scalar(dst[:, t, :], src[:, t, :], mv[k][:, t, 0:1], rstd[k][:, t:t + 1],
                                      ALU.subtract, ALU.mult).then_inc(s_done, 1)

            def body(s):
                u, v, z = wide[s.off % 2], wide[1 - s.off % 2], wide[2]
                b0, b1, b2, b3, b4, b5 = (s.seq(k) for k in range(6))
                if s.active(2):
                    wait(dve, s_spq, 4 * b2)
                    dve.wait_ge(s_cq, 2 * b2 + 1)
                    maxima(u, nmax_q, 0, s_maxq)
                    dve.wait_ge(s_cq, 2 * b2 + 2)
                    maxima(z, nmax_q, 1, s_maxq)
                if s.active(4):
                    stats(2, b4, [x1[s.par(4)][:, t, :] for t in range(NT)], [(s_x1, b4 + 1)])
                if s.active(3):
                    dve.wait_ge(s_kv, b3 + 1)
                    wait(dve, s_trkv, b3)
                    for r in range(NR):
                        dve.scalar_tensor_tensor(kvt[:, r, :], m1[:, r * MW:r * MW + 2 * M],
                                                 m1[:, r * MW + 2 * M:(r + 1) * MW], kv_mask, ALU.add, ALU.mult,
                                                 accum_out=kv_sum[:, r:r + 1]).then_inc(s_kvt, 1)
                    dve.wait_ge(s_kvt, 2 * b3 + 2)
                    wait(dve, s_outt, 2 * b3)
                    dve.tensor_scalar(kv_sum8[:, :], kv_sum[:, :], EPS8, None, ALU.mult).then_inc(s_kvsum, 1)
                if s.active(1):
                    dve.wait_ge(s_hi, 2 * b1 + 2)
                    for j in range(2):
                        dve.scalar_tensor_tensor(lo[:, j, :], m0[:, j * N:(j + 1) * N], bq[:, j:j + 1],
                                                 hi[:, j, :], ALU.add, ALU.subtract).then_inc(s_lo, 1)
                if s.active(4):
                    normalize(2, b4, xn2, x1[s.par(4)], s_xn2, s_x2t)
                if s.active(2):
                    wait(dve, s_spk, 8 * b2)
                    dve.wait_ge(s_ck, 2 * b2 + 1)
                    maxima(v, nmax_k, 0, s_maxk)
                if s.active(0):
                    p = s.par(0)
                    stats(0, b0, [xin[p][:, t, :] for t in range(NT)], [(s_xin[p], 16 * (s.round(0) + 1))])
                if s.active(2):
                    dve.wait_ge(s_ck, 2 * b2 + 2)
                    maxima(u, nmax_k, 1, s_maxk)
                if s.active(1):
                    p = s.par(1)
                    dve.wait_ge(s_v, b1 + 1)
                    wait(dve, s_kv, b1 - 1)
                    for h in range(2):
                        dve.tensor_tensor(vaug[p][:, :, :, h * VW:h * VW + HD],
                                          m0[:, 0:NT * D].rearrange("p (t n d) -> p t n d", t=NT, n=NP)
                                          [:, :, :, h * HD:(h + 1) * HD],
                                          bv[:, :, :].rearrange("p t (n d) -> p t n d", n=NP)
                                          [:, :, :, h * HD:(h + 1) * HD], ALU.add).then_inc(s_vsb, 1)
                if s.active(0):
                    normalize(0, b0, xn, xin[s.par(0)], s_xn, s_xt)
                if s.active(3):
                    dve.wait_ge(s_trout, b3 + 1)
                    o = m1[:, :].rearrange("p (n c) -> p n c", c=PW)[:, :, 0:2 * VW].rearrange(
                        "p n (h c) -> p n h c", h=2)
                    dve.tensor_scalar(den[:, :].rearrange("p (n h) -> p n h", h=2), o[:, :, :, HD],
                                      64.0 * EPS_FAVOR, None, ALU.add).then_inc(s_den, 1)
                    dve.wait_ge(s_den, b3 + 1)
                    dve.reciprocal(rden[:, :], den[:, :]).then_inc(s_rden, 1)
                    dve.wait_ge(s_rden, b3 + 1)
                    wait(dve, s_attt, b3)
                    dve.tensor_tensor(att[:, :, :].rearrange("p (n h) d -> p n h d", h=2), o[:, :, :, 0:HD],
                                      rden[:, :].rearrange("p (n h) -> p n h", h=2).unsqueeze(3)
                                      .broadcast_to([P, NT * NP, 2, HD]), ALU.mult).then_inc(s_att, 1)
                if s.active(5):
                    dve.wait_ge(s_ysb, b5 + 1)
                    wait(dve, s_cn, 2 * b5)
                    y = y_sb[:, :]
                    dve.tensor_scalar(cnt[0][:, :], y, thresholds[0], None, ALU.is_gt).then_inc(s_cnt, 1)
                    for n in range(1, NUM_STEPS):
                        dve.wait_ge(s_cnt, NUM_STEPS * b5 + n)
                        dve.scalar_tensor_tensor(cnt[n % 2][:, :], y, thresholds[n], cnt[1 - n % 2][:, :],
                                                 ALU.is_gt, ALU.add).then_inc(s_cnt, 1)
                    stats(3, b5, [cnt[0][:, t * D:(t + 1) * D] for t in range(NT)],
                          [(s_cnt, NUM_STEPS * (b5 + 1))])
                if s.active(3):
                    dve.wait_ge(s_proj, b3 + 1)
                    wait(dve, s_x1n, 2 * b3)
                    dve.tensor_tensor(a_sb[:, :, :], m1[:, 0:NT * D].rearrange("p (t d) -> p t d", t=NT),
                                      bp[:, :, :], ALU.add).then_inc(s_a, 1)
                    stats(1, b3, [a_sb[:, t, :] for t in range(NT)], [(s_a, b3 + 1)])

            slots(dve, body)


_INS = ['L0_attn_x', 'L0_attn_qkv_w', 'L0_attn_qkv_b', 'L0_attn_proj_w', 'L0_attn_proj_b',
        'L0_attn_projection_matrix', 'L0_ffn_W_fc', 'L0_ffn_W_proj']


def kernel(**inputs):
    import numpy as _np
    import concourse.bacc as _bacc
    from concourse import mybir as _mybir
    from concourse.bass_utils import run_bass_kernel_spmd as _run

    rows = _np.arange(128)
    const = _np.zeros((128, 128 + 4 + 2 + 128), _np.float32)
    const[rows, rows] = 1
    const[rows, 128 + rows % 32 // 8] = 1
    const[rows, 132 + rows // 32 % 2] = 1
    for head in range(2):
        const[rows % 32 // 9 == head, 134 + 64 * head:134 + 64 * (head + 1)] = 1
    indicator = _np.zeros((128, 16, 64), _np.float16)
    for part in range(3):
        indicator[16 * part + _np.arange(16), _np.arange(16)] = 1

    nc = _bacc.Bacc("TRN2", target_bir_lowering=False, num_devices=1)
    arrays, args = {}, []
    named = {**{name: inputs[name] for name in _INS}, "const": const, "indicator": indicator.reshape(128, 1024)}
    for name, value in named.items():
        a = _np.ascontiguousarray(value)
        arrays[f"in_{name}_dram"] = a
        args.append(nc.dram_tensor(f"in_{name}_dram", a.shape, _mybir.dt.from_np(a.dtype), kind="ExternalInput").ap())
    shape = inputs["L0_attn_x"].shape
    args.append(nc.dram_tensor("out_0_dram", shape, _mybir.dt.float32, kind="ExternalOutput").ap())
    sandwich_kernel(nc, *args)
    r = _run(nc, [arrays], core_ids=[0])
    return r.results[0]["out_0_dram"]
```

```python
from contextlib import ExitStack

import concourse.bass as bass
from concourse import mybir

F32 = mybir.dt.float32
F16 = mybir.dt.float16
BF16 = mybir.dt.bfloat16
ALU = mybir.AluOpType
ACT = mybir.ActivationFunctionType
AX_X = mybir.AxisListType.X

P = 128
EPS_LN = 1e-5
EPS_FAVOR = 1e-6
BETA = 0.9
NUM_STEPS = 5
SPLIT_SCALE = 64.0


def spike_thresholds():
    def spikes(y):
        m, n = 0.0, 0
        for _ in range(NUM_STEPS):
            m = BETA * m + y - (1.0 if m > 1.0 else 0.0)
            n += m > 1.0
        return n

    edges = []
    for n in range(1, NUM_STEPS + 1):
        low, high = 0.0, 4.0
        for _ in range(80):
            mid = (low + high) / 2
            low, high = (low, mid) if spikes(mid) >= n else (mid, high)
        edges.append(high)
    return edges


def sandwich_kernel(nc, x, qkv_w, qkv_b, proj_w, proj_b, pm, w_fc, w_proj, const, indicator, out):
    NB, N, D = x.shape
    M, HD = pm.shape
    H = D // HD
    FF = w_fc.shape[0]
    NT = N // P
    NG = P // 32
    HG = H // NG
    GW = HG * M
    NP = H // 2
    VW = HD + 1
    PW = 32
    MW = 2 * M + 1
    NR = NP // 4
    FC = FF // P
    HM = H * M
    EXP_SCALE = 1.0 / (SPLIT_SCALE * SPLIT_SCALE * float(HD) ** 0.5)
    EPS8 = 8.0 * EPS_FAVOR
    assert NT == 2 and HM == 1024 and FF == 512 and M == 64 and NB % 2 == 0
    thresholds = spike_thresholds()

    x_v = x.rearrange("b (t p) d -> b p t d", p=P)
    out_v = out.rearrange("b (t p) d -> b p t d", p=P)

    with ExitStack() as ctx:
        def sb(name, shape, dt=F32):
            return ctx.enter_context(nc.sbuf_tensor(name, shape, dt))

        def sem(name):
            return ctx.enter_context(nc.semaphore(name))

        cst = sb("cst", [P, P + HG + 2 + P])
        ident = cst[:, 0:P]
        head_mask = cst[:, P:P + HG]
        kv_mask = cst[:, P + HG + 2:]
        ident_bf = sb("ident_bf", [P, P], BF16)
        ind = sb("ind", [P, HM], F16)
        neg_half = sb("neg_half", [P, NT])
        w_raw = sb("w_raw", [P, 3 + 1 + FC + FC, P])
        pm16 = sb("pm16", [M, 4 * HG, HD])
        pm_raw = sb("pm_raw", [M, HD])
        bq_raw = sb("bq_raw", [P, 2])
        bq = sb("bq", [P, 2])
        bv = sb("bv", [P, NT, D])
        bp = sb("bp", [P, NT, D])
        wqk_t = sb("wqk_t", [P, 2, D])
        wv_t = sb("wv_t", [P, D])
        wp_t = sb("wp_t", [P, D])
        wfc_t = sb("wfc_t", [P, FC, P])
        wpr_t = sb("wpr_t", [P, FC, D])
        pf = sb("pf", [P, HG, M])
        pf_hi = sb("pf_hi", [P, HG, M], F16)
        pf_lo = sb("pf_lo", [P, HG, M], F16)
        pst_a = sb("pst_a", [P, HG * M], F16)
        pst = sb("pst", [P, HG * M], F16)

        xin = [sb(f"xin{i}", [P, NT, D]) for i in range(2)]
        xres = sb("xres", [P, NT, D])
        xn = sb("xn", [P, NT, D])
        xn_t = sb("xn_t", [P, N])
        hi = sb("hi", [P, 2, N], F16)
        lo = sb("lo", [P, 2, N], F16)
        stack = [sb(f"stack{i}", [P, NG, 2, N], F16) for i in range(2)]
        vaug = [sb(f"vaug{i}", [P, NT, NP, PW]) for i in range(2)]
        nmax_q = sb("nmax_q", [P, NT, H])
        nmax_k = sb("nmax_k", [P, NT, H])
        rem_q = sb("rem_q", [P, NT, H])
        rem_k = sb("rem_k", [P, NT, H])
        parts_q = sb("parts_q", [P, NT, P], BF16)
        parts_k = sb("parts_k", [P, NT, P], BF16)
        parts_qt = sb("parts_qt", [P, N], BF16)
        parts_kt = sb("parts_kt", [P, N], BF16)
        ek = sb("ek", [P, NT, NP, MW])
        eq_t = sb("eq_t", [P, NP, N])
        kvt = sb("kvt", [P, NR, P])
        kv_sum = sb("kv_sum", [P, NR])
        kv_sum8 = sb("kv_sum8", [P, NR])
        kvb = sb("kvb", [P, NP, PW])
        out_t = sb("out_t", [P, NR, N])
        den = sb("den", [P, NT * H])
        rden = sb("rden", [P, NT * H])
        att = sb("att", [P, NT * H, HD])
        att_t = sb("att_t", [P, N])
        a_sb = sb("a_sb", [P, NT, D])
        x1 = [sb(f"x1_{i}", [P, NT, D]) for i in range(2)]
        x1n = sb("x1n", [P, NT, D])
        xn2 = sb("xn2", [P, NT, D])
        xn2_t = sb("xn2_t", [P, N])
        y_sb = sb("y_sb", [P, NT * D])
        relu = sb("relu", [P, FC, N])
        hsq = sb("hsq", [P, FC, N])
        cnt = [sb(f"cnt{i}", [P, NT * D]) for i in range(2)]
        cn = sb("cn", [P, NT, D])
        xo = sb("xo", [P, NT, D])
        st = [sb(f"st{k}", [P, NT, 6]) for k in range(4)]
        mv = [sb(f"mv{k}", [P, NT, 2]) for k in range(4)]
        var = [sb(f"var{k}", [P, NT]) for k in range(4)]
        nmean = [sb(f"nmean{k}", [P, NT]) for k in range(4)]
        rstd = [sb(f"rstd{k}", [P, NT]) for k in range(4)]
        shift = {k: sb(f"shift{k}", [P, NT]) for k in (0, 2)}

        wide = [ctx.enter_context(nc.psum_tensor(f"wide{i}", [P, HM], F32)) for i in range(3)]
        m0 = ctx.enter_context(nc.psum_tensor("m0", [P, 512], F32))
        m1 = ctx.enter_context(nc.psum_tensor("m1", [P, 512], F32))

        parts_dram = [nc.dram_tensor(f"parts_dram{i}", [2, P, 2 * N], F16).ap() for i in range(2)]

        s_settled = {nc.vector: sem("s_settled_dve"), nc.gpsimd: sem("s_settled_pool"),
                     nc.sync: sem("s_settled_sp")}
        s_first = sem("s_first")
        s_const = sem("s_const")
        s_zero = sem("s_zero")
        s_wtr = sem("s_wtr")
        s_wcopy = sem("s_wcopy")
        s_prep = sem("s_prep")
        s_pmrep = sem("s_pmrep")
        s_xin = [sem("s_xin0"), sem("s_xin1")]
        s_xres = sem("s_xres")
        s_stat = [sem(f"s_stat{k}") for k in range(4)]
        s_mv = [sem(f"s_mv{k}") for k in range(4)]
        s_var = [sem(f"s_var{k}") for k in range(4)]
        s_rstd = [sem(f"s_rstd{k}") for k in range(4)]
        s_shift = {k: sem(f"s_shift{k}") for k in (0, 2)}
        s_xn = sem("s_xn")
        s_xt = sem("s_xt")
        s_xnt = sem("s_xnt")
        s_qk = sem("s_qk")
        s_hi = sem("s_hi")
        s_lo = sem("s_lo")
        s_hi_dram = [sem("s_hi_dram0"), sem("s_hi_dram1")]
        s_lo_dram = [sem("s_lo_dram0"), sem("s_lo_dram1")]
        s_stack = [sem("s_stack0"), sem("s_stack1")]
        s_v = sem("s_v")
        s_vsb = sem("s_vsb")
        s_cq = sem("s_cq")
        s_ck = sem("s_ck")
        s_maxq = sem("s_maxq")
        s_maxk = sem("s_maxk")
        s_spq = sem("s_spq")
        s_spk = sem("s_spk")
        s_ptq = sem("s_ptq")
        s_ptk = sem("s_ptk")
        s_ptq_sb = sem("s_ptq_sb")
        s_ptk_sb = sem("s_ptk_sb")
        s_qt = sem("s_qt")
        s_ksub = sem("s_ksub")
        s_expq = sem("s_expq")
        s_expk = sem("s_expk")
        s_kv = sem("s_kv")
        s_kvt = sem("s_kvt")
        s_kvsum = sem("s_kvsum")
        s_trkv = sem("s_trkv")
        s_kvb = sem("s_kvb")
        s_outt = sem("s_outt")
        s_out = sem("s_out")
        s_trout = sem("s_trout")
        s_den = sem("s_den")
        s_rden = sem("s_rden")
        s_att = sem("s_att")
        s_attt = sem("s_attt")
        s_attt_sb = sem("s_attt_sb")
        s_proj = sem("s_proj")
        s_a = sem("s_a")
        s_x1n = sem("s_x1n")
        s_x1 = sem("s_x1")
        s_xn2 = sem("s_xn2")
        s_x2t = sem("s_x2t")
        s_xn2t = sem("s_xn2t")
        s_ff1 = sem("s_ff1")
        s_relu = sem("s_relu")
        s_hsq = sem("s_hsq")
        s_y = sem("s_y")
        s_ysb = sem("s_ysb")
        s_cnt = sem("s_cnt")
        s_cn = sem("s_cn")
        s_xo = sem("s_xo")
        s_store = sem("s_store")

        def wait(eng, s, value):
            if not isinstance(value, int) or value > 0:
                eng.wait_ge(s, value)

        def settle(eng):
            eng.sem_inc(s_settled[eng], 1)

        class Slot:

            def __init__(self, half, off):
                self.half, self.base, self.off = half, half * 2, off

            def seq(self, k):
                return self.base + (self.off - k)

            def par(self, k):
                return (self.off - k) % 2

            def round(self, k):
                return self.half + (self.off - k - self.par(k)) // 2

            def first(self, k):
                return isinstance(self.base, int) and self.seq(k) == 0

            def active(self, k):
                return not isinstance(self.base, int) or 0 <= self.seq(k) < NB

        STAGES = 6
        PEELED = 6
        LAST = NB + STAGES - 1

        def slots(eng, body):
            for t in range(PEELED):
                body(Slot(t // 2, t % 2))
            with eng.Fori(PEELED // 2, NB // 2) as i:
                for off in range(2):
                    body(Slot(i, off))
            for t in range(NB, LAST):
                body(Slot(t // 2, t % 2))

        def done(value):
            return min(value, NB) if isinstance(value, int) else value

        block = ctx.enter_context(nc.Block())

        N_FIRST = 4
        N_CONST = 8
        ZEROED = 10

        @block.sync
        def _(sp):
            sp.dma_start(cst[:, :], const).then_inc(s_first, 16)
            sp.dma_start(w_raw[:, 0:3, :], qkv_w.rearrange("(c p) d -> p c d", p=P)).then_inc(s_first, 16)
            sp.dma_start(pm_raw[:, :], pm).then_inc(s_first, 16)
            with nc.allow_non_contiguous_dma(reason="two short bias columns"):
                sp.dma_start(bq_raw[:, :], qkv_b[0:2 * D].rearrange("(c p) -> p c", p=P)).then_inc(s_first, 16)

            def other_constants():
                for t in range(NT):
                    sp.dma_start(bv[:, t, :], qkv_b[2 * D:3 * D].rearrange("(a d) -> a d", a=1)
                                 .broadcast_to([P, D])).then_inc(s_const, 16)
                sp.dma_start(w_raw[:, 3, :], proj_w).then_inc(s_const, 16)
                sp.dma_start(w_raw[:, 4:4 + FC, :], w_fc.rearrange("(c p) d -> p c d", p=P)).then_inc(s_const, 16)
                sp.dma_start(w_raw[:, 4 + FC:, :], w_proj.rearrange("d (c f) -> d c f", c=FC)).then_inc(s_const, 16)
                sp.dma_start(ind[:, :], indicator).then_inc(s_const, 16)
                for t in range(NT):
                    sp.dma_start(bp[:, t, :], proj_b.rearrange("(a d) -> a d", a=1)
                                 .broadcast_to([P, D])).then_inc(s_const, 16)

            def stack_part(p, part):
                for r in range(2):
                    row = 64 * part + 32 * r
                    sp.dma_start(stack[p][row:row + 32, :, :, :].rearrange("p g j n -> p g (j n)"),
                                 parts_dram[p][part].rearrange("(g p) n -> p g n", p=32)).then_inc(s_stack[p], 16)

            def body(s):
                b0, b1, b2, b3, b4, b5 = (s.seq(k) for k in range(6))
                if s.active(4):
                    wait(sp, s_x1, b4)
                    sp.dma_start(xres[:, :, :], x_v[b4]).then_inc(s_xres, 16)
                if s.active(2):
                    p = s.par(2)
                    wait(sp, s_hi, 2 * b2 + 2)
                    settle(sp)
                    wait(sp, s_stack[p], 16 * 4 * s.round(2))
                    sp.dma_start(parts_dram[p][0], hi[:, :, :].rearrange("p j n -> p (j n)")).then_inc(s_hi_dram[p], 16)
                if s.active(0):
                    p = s.par(0)
                    wait(sp, s_xn, 2 * (b0 - 1))
                    sp.dma_start(xin[p][:, :, :], x_v[b0]).then_inc(s_xin[p], 16)
                if s.active(2):
                    p = s.par(2)
                    wait(sp, s_lo, 2 * b2 + 2)
                    sp.dma_start(parts_dram[p][1], lo[:, :, :].rearrange("p j n -> p (j n)")).then_inc(s_lo_dram[p], 16)
                if s.first(1):
                    other_constants()
                if s.active(2):
                    p = s.par(2)
                    wait(sp, s_qt, 2 * (b2 - 1))
                    wait(sp, s_ck, 2 * (b2 - 1))
                    settle(sp)
                    sp.wait_ge(s_hi_dram[p], 16 * (s.round(2) + 1))
                    stack_part(p, 0)
                    p = s.par(2)
                    sp.wait_ge(s_lo_dram[p], 16 * (s.round(2) + 1))
                    stack_part(p, 1)
                if s.active(5):
                    sp.wait_ge(s_xo, b5 + 1)
                    sp.dma_start(out_v[b5], xo[:, :, :]).then_inc(s_store, 16)

            slots(sp, body)
            sp.wait_ge(s_store, 16 * NB)

        @block.gpsimd
        def _(pool):
            pool.memset(parts_q[:, :, :], 0.0).then_inc(s_zero, 1)
            pool.memset(parts_k[:, :, :], 0.0).then_inc(s_zero, 1)
            for i in range(2):
                pool.memset(vaug[i][:, :, :, :], 0.0).then_inc(s_zero, 1)
            pool.memset(ek[:, :, :, 2 * M:MW], EPS8).then_inc(s_zero, 1)
            pool.memset(neg_half[:, :], -0.5).then_inc(s_zero, 1)
            pool.wait_ge(s_zero, 6)
            for i in range(2):
                for h in range(2):
                    c = h * VW + HD
                    pool.memset(vaug[i][:, :, :, c:c + 1], 1.0).then_inc(s_zero, 1)
            pool.wait_ge(s_zero, ZEROED)

            def inv_std(k, b, eps, last_readers):
                for sm, value in last_readers:
                    wait(pool, sm, value)
                pool.wait_ge(s_mv[k], 2 * b + 2)
                settle(pool)
                pool.tensor_scalar(var[k][:, :], mv[k][:, :, 1], eps, None, ALU.add).then_inc(s_var[k], 1)
                pool.tensor_scalar(nmean[k][:, :], mv[k][:, :, 0], -1.0, None, ALU.mult).then_inc(s_var[k], 1)
                pool.wait_ge(s_var[k], 2 * b + 2)
                pool.tensor_tensor(rstd[k][:, :], var[k][:, :], neg_half[:, :], ALU.pow).then_inc(s_rstd[k], 1)
                if k in (0, 2):
                    pool.wait_ge(s_rstd[k], b + 1)
                    pool.tensor_tensor(shift[k][:, :], nmean[k][:, :], rstd[k][:, :], ALU.mult).then_inc(s_shift[k], 1)

            def normalize(k, t, dst, src, done_sem):
                settle(pool)
                pool.tensor_scalar(dst, src, nmean[k][:, t:t + 1], rstd[k][:, t:t + 1], ALU.add,
                                   ALU.mult).then_inc(done_sem, 1)

            def split(nm, rem, parts, lo_t, hi_t, s_split, first):
                n = nm[:, lo_t:hi_t, :]
                r = rem[:, lo_t:hi_t, :]
                a = [parts[:, lo_t:hi_t, H * i:H * (i + 1)] for i in range(3)]
                settle(pool)
                pool.tensor_copy(a[0], n).then_inc(s_split, 1)
                pool.wait_ge(s_split, first + 1)
                pool.tensor_tensor(r, n, a[0], ALU.subtract).then_inc(s_split, 1)
                pool.wait_ge(s_split, first + 2)
                settle(pool)
                pool.tensor_copy(a[1], r).then_inc(s_split, 1)
                pool.wait_ge(s_split, first + 3)
                pool.tensor_tensor(a[2], r, a[1], ALU.subtract).then_inc(s_split, 1)

            def body(s):
                b0, b1, b2, b3, b4, b5 = (s.seq(k) for k in range(6))
                if s.active(3):
                    split_k(b3, 0)
                if s.active(1):
                    inv_std(0, b1, EPS_LN, [(s_xn, 2 * b1)])
                if s.active(3):
                    split_k(b3, 1)
                if s.active(4):
                    inv_std(1, b4, EPS_LN, [])
                    pool.wait_ge(s_rstd[1], b4 + 1)
                    for t in range(NT):
                        normalize(1, t, x1n[:, t, :], a_sb[:, t, :], s_x1n)
                    pool.wait_ge(s_x1n, 2 * b4 + 2)
                    pool.wait_ge(s_xres, 16 * (b4 + 1))
                    wait(pool, s_xo, b4 - 1)
                    pool.tensor_tensor(x1[s.par(4)][:, :, :], x1n[:, :, :], xres[:, :, :], ALU.add).then_inc(s_x1, 1)
                    inv_std(2, b4, EPS_LN, [(s_xn2, 2 * b4)])
                if s.active(5):
                    inv_std(3, b5, EPS_LN * NUM_STEPS * NUM_STEPS, [])
                    pool.wait_ge(s_rstd[3], b5 + 1)
                    for t in range(NT):
                        normalize(3, t, cn[:, t, :], cnt[0][:, t * D:(t + 1) * D], s_cn)
                    pool.wait_ge(s_cn, 2 * b5 + 2)
                    wait(pool, s_store, 16 * b5)
                    pool.tensor_tensor(xo[:, :, :], cn[:, :, :], x1[s.par(5)][:, :, :], ALU.add).then_inc(s_xo, 1)
                if s.active(2):
                    pool.wait_ge(s_maxq, 2 * b2 + 2)
                    wait(pool, s_ptq, b2)
                    split(nmax_q, rem_q, parts_q, 0, NT, s_spq, 4 * b2)

            def split_k(b, t):
                pool.wait_ge(s_maxk, 2 * b + t + 1)
                if t == 0:
                    wait(pool, s_ptk, 2 * b)
                split(nmax_k, rem_k, parts_k, t, t + 1, s_spk, 8 * b + 4 * t)

            slots(pool, body)

        @block.scalar
        def _(act):
            act.wait_ge(s_first, 16 * N_FIRST)
            act.activation(bq[:, :], bq_raw[:, :], ACT.Copy, scale=SPLIT_SCALE).then_inc(s_wcopy, 1)
            act.wait_ge(s_wtr, 1)
            act.activation(wqk_t[:, :, :], wide[0][:, 0:2 * P].rearrange("p (c d) -> p c d", c=2), ACT.Copy,
                           scale=SPLIT_SCALE).then_inc(s_wcopy, 1)
            act.activation(wv_t[:, :], wide[0][:, 2 * P:3 * P], ACT.Copy).then_inc(s_wcopy, 1)
            act.activation(ident_bf[:, :], ident, ACT.Copy).then_inc(s_wcopy, 1)

            def other_weights():
                act.wait_ge(s_wtr, 3)
                act.activation(wfc_t[:, :, :], wide[1][:, 0:FC * P].rearrange("p (c d) -> p c d", c=FC),
                               ACT.Copy).then_inc(s_wcopy, 1)
                act.wait_ge(s_wtr, 4)
                act.activation(wpr_t[:, :, :], wide[2][:, 0:FC * P].rearrange("p (c d) -> p c d", c=FC),
                               ACT.Copy).then_inc(s_wcopy, 1)
                act.wait_ge(s_wtr, 5)
                act.activation(wp_t[:, :], wide[0][:, 0:P], ACT.Copy).then_inc(s_wcopy, 1)

            def body(s):
                b0, b1, b2, b3, b4, b5 = (s.seq(k) for k in range(6))
                if s.active(2):
                    p = s.par(2)
                    act.wait_ge(s_qk, b2 + 1)
                    for stored in (s_hi_dram, s_lo_dram):
                        wait(act, stored[1 - p], 16 * (s.round(2) + p))
                    for j in range(2):
                        act.activation(hi[:, j, :], m0[:, j * N:(j + 1) * N], ACT.Identity,
                                       bias=bq[:, j:j + 1]).then_inc(s_hi, 1)
                if s.active(4):
                    exp_q(b4, 1)
                if s.active(5):
                    normalize(2, b5, xn2, x1[s.par(5)], s_xn2, s_x2t)
                if s.active(4):
                    act.wait_ge(s_trkv, b4 + 1)
                    wait(act, s_out, b4)
                    act.activation(kvb[:, :, :], m1[:, 0:NP * PW].rearrange("p (n c) -> p n c", n=NP),
                                   ACT.Copy).then_inc(s_kvb, 1)
                if s.active(5):
                    act.wait_ge(s_x2t, b5 + 1)
                    wait(act, s_ff1, b5)
                    act.activation(xn2_t[:, :], m0[:, 0:N], ACT.Copy).then_inc(s_xn2t, 1)
                if s.active(4):
                    act.wait_ge(s_out, b4 + 1)
                    wait(act, s_trout, b4)
                    act.wait_ge(s_kvsum, b4 + 1)
                    for r in range(NR):
                        act.activation(out_t[:, r, :], m1[:, r * N:(r + 1) * N], ACT.Identity,
                                       bias=kv_sum8[:, r:r + 1]).then_inc(s_outt, 1)
                if s.first(2):
                    other_weights()
                if s.active(5):
                    act.wait_ge(s_ff1, b5 + 1)
                    act.activation(relu[:, :, :], wide[2][:, :].rearrange("p (c n) -> p c n", c=FC),
                                   ACT.Relu).then_inc(s_relu, 1)
                if s.active(3):
                    act.wait_ge(s_ptq, b3 + 1)
                    wait(act, s_qt, 2 * b3)
                    act.activation(parts_qt[:, :], m0[:, 0:N // 2].bitcast(BF16), ACT.Copy).then_inc(s_ptq_sb, 1)
                if s.active(5):
                    act.wait_ge(s_relu, b5 + 1)
                    wait(act, s_y, b5)
                    act.activation(hsq[:, :, :], relu[:, :, :], ACT.Square).then_inc(s_hsq, 1)
                if s.active(4):
                    act.wait_ge(s_attt, b4 + 1)
                    wait(act, s_proj, b4)
                    act.activation(att_t[:, :], m1[:, 0:N], ACT.Copy).then_inc(s_attt_sb, 1)
                if s.active(3):
                    copy_parts_k(m0, b3, 0)
                if s.active(1):
                    normalize(0, b1, xn, xin[s.par(1)], s_xn, s_xt)
                if s.active(3):
                    exp_q(b3, 0)
                if s.active(5):
                    act.wait_ge(s_y, b5 + 1)
                    wait(act, s_cnt, NT * NUM_STEPS * b5)
                    act.activation(y_sb[:, :], m0[:, 0:NT * D], ACT.Copy).then_inc(s_ysb, 1)
                if s.active(3):
                    copy_parts_k(m1, b3, 1)
                if s.active(1):
                    act.wait_ge(s_xt, b1 + 1)
                    wait(act, s_v, b1)
                    act.activation(xn_t[:, :], m0[:, 0:N], ACT.Copy).then_inc(s_xnt, 1)
                if s.active(3):
                    exp_k(s, 3, 0)
                    exp_k(s, 3, 1)

            def normalize(k, b, dst, src, s_done, last_reader):
                act.wait_ge(s_shift[k], b + 1)
                wait(act, last_reader, b)
                for t in range(NT):
                    act.activation(dst[:, t, :], src[:, t, :], ACT.Identity, bias=shift[k][:, t:t + 1],
                                   scale=rstd[k][:, t:t + 1]).then_inc(s_done, 1)

            def copy_parts_k(m, b, t):
                act.wait_ge(s_ptk, 2 * b + t + 1)
                wait(act, s_ksub, 2 * b + t - 1)
                act.activation(parts_kt[:, t * P:(t + 1) * P], m[:, 0:P // 2].bitcast(BF16),
                               ACT.Copy).then_inc(s_ptk_sb, 1)

            def exp_q(b, j):
                act.wait_ge(s_qt, 2 * b + j + 1)
                if j == 0:
                    wait(act, s_out, b)
                act.activation(eq_t[:, 4 * j:4 * j + 4, :], wide[2][:, :].rearrange("p (c n) -> p c n", c=4),
                               ACT.Exp, scale=EXP_SCALE).then_inc(s_expq, 1)

            def exp_k(s, lag, t):
                b = s.seq(lag)
                w = wide[(1 - s.par(lag) + t) % 2]
                act.wait_ge(s_ksub, 2 * b + t + 1)
                wait(act, s_kv, b)
                act.activation(ek[:, t, :, 0:2 * M], w[:, :].rearrange("p (n c) -> p n c", n=NP), ACT.Exp,
                               scale=EXP_SCALE).then_inc(s_expk, 1)

            slots(act, body)

        @block.tensor
        def _(pe):
            pe.wait_ge(s_first, 16 * N_FIRST)
            for c in range(3):
                mm = pe.transpose(wide[0][:, c * P:(c + 1) * P], w_raw[:, c, :], ident)
            mm.then_inc(s_wtr, 1)
            pe.wait_ge(s_pmrep, 1)
            pe.matmul(wide[0][:, 512:512 + M], pm16[:, :, :].rearrange("m r d -> m (r d)"), cst[0:M, 0:M], start=True,
                      stop=True).then_inc(s_wtr, 1)
            pe.wait_ge(s_wcopy, 4)

            def other_weights():
                pe.wait_ge(s_const, 16 * N_CONST)
                for c in range(FC):
                    mm = pe.transpose(wide[1][:, c * P:(c + 1) * P], w_raw[:, 4 + c, :], ident)
                mm.then_inc(s_wtr, 1)
                for c in range(FC):
                    mm = pe.transpose(wide[2][:, c * P:(c + 1) * P], w_raw[:, 4 + FC + c, :], ident)
                mm.then_inc(s_wtr, 1)
                pe.transpose(wide[0][:, 0:P], w_raw[:, 3, :], ident).then_inc(s_wtr, 1)

            def all_prepared():
                pe.wait_ge(s_wcopy, 7)
                pe.wait_ge(s_prep, 1)
                pe.wait_ge(s_zero, ZEROED)

            def features(s, lag, j, t, w, done_sem):
                p = s.par(lag)
                for g in range(NG):
                    mm = pe.matmul(w[:, g * GW:(g + 1) * GW], stack[p][:, g, j, t * P:(t + 1) * P], pst[:, :],
                                   start=(g % 2 == 0), stop=False, skip_group_check=True)
                mm.then_inc(done_sem, 1)

            def features_t(s, lag, half):
                p = s.par(lag)
                for i in range(NP // 2):
                    pair = half * (NP // 2) + i
                    g, e = pair // 2, pair % 2
                    o = wide[2][:, i * N:(i + 1) * N]
                    pe.matmul(o, pst[:, e * P:(e + 1) * P], stack[p][:, g, 0, :],
                              start=(i % 2 == 0), stop=False, skip_group_check=True)
                    mm = pe.matmul(o, ind[:, pair * P:(pair + 1) * P], parts_qt[:, :], start=False,
                                   stop=True, skip_group_check=True)
                mm.then_inc(s_qt, 1)

            def parts_k_t(m, t):
                pe.transpose(m[:, 0:P // 2].bitcast(BF16), parts_k[:, t, :], ident_bf[:, :]).then_inc(s_ptk, 1)

            def sub_max_k(s, lag, t):
                b = s.seq(lag)
                w = wide[(1 - s.par(lag) + t) % 2]
                pe.wait_ge(s_ptk_sb, 2 * b + t + 1)
                for c in range(2):
                    mm = pe.matmul(w[:, c * 512:(c + 1) * 512], parts_kt[:, t * P:(t + 1) * P],
                                   ind[:, c * 512:(c + 1) * 512], start=False, stop=True, skip_group_check=True)
                mm.then_inc(s_ksub, 1)

            def body(s):
                b0, b1, b2, b3, b4, b5 = (s.seq(k) for k in range(6))
                if s.active(4):
                    sub_max_k(s, 4, 0)
                    pe.wait_ge(s_spk, 8 * b4 + 8)
                    wait(pe, s_a, b4)
                    parts_k_t(m1, 1)
                if s.active(2):
                    pe.wait_ge(s_xn, 2 * b2 + 2)
                    wait(pe, s_ysb, b5)
                    wait(pe, s_ptk_sb, 2 * b3 - 1)
                    wait(pe, s_vsb, 2 * b2)
                    for t in range(NT):
                        mm = pe.transpose(m0[:, t * P:(t + 1) * P], xn[:, t, :], ident)
                    mm.then_inc(s_xt, 1)
                if s.active(4):
                    sub_max_k(s, 4, 1)
                if s.first(3):
                    all_prepared()
                if s.active(2):
                    pe.wait_ge(s_xnt, b2 + 1)
                    for j in range(2):
                        mm = pe.matmul(m0[:, j * N:(j + 1) * N], wqk_t[:, j, :], xn_t[:, :], start=True, stop=True)
                    mm.then_inc(s_qk, 1)
                if s.first(2):
                    other_weights()
                if s.active(4):
                    wait(pe, s_expq, 2 * b3 - 1)
                    features_t(s, 4, 1)
                    p = s.par(4)
                    pe.wait_ge(s_vsb, 2 * b4 + 2)
                    wait(pe, s_ptk_sb, 2 * (b4 + 1))
                    for t in range(NT):
                        pe.wait_ge(s_expk, 2 * b4 + t + 1)
                        for n in range(NP):
                            c, r = n % 4, n // 4
                            mm = pe.matmul(m1[c * PW:(c + 1) * PW, r * MW:(r + 1) * MW], vaug[p][:, t, n, :],
                                           ek[:, t, n, :], start=(t == 0 and r == 0), stop=(t == NT - 1),
                                           tile_position=(0, c * PW), skip_group_check=True)
                    mm.then_inc(s_kv, 1)
                if s.active(3):
                    pe.wait_ge(s_stack[s.par(3)], 16 * 4 * (s.round(3) + 1))
                    wait(pe, s_expk, 2 * b3 - 1)
                    features(s, 3, 0, 0, wide[s.par(3)], s_cq)
                    wait(pe, s_expq, 2 * (b4 + 1))
                    features(s, 3, 0, 1, wide[2], s_cq)
                if s.active(4):
                    pe.wait_ge(s_kvt, 2 * b4 + 2)
                    for r in range(NR):
                        mm = pe.transpose(m1[:, r * P:(r + 1) * P], kvt[:, r, :], ident)
                    mm.then_inc(s_trkv, 1)
                if s.active(3):
                    wait(pe, s_expk, 2 * b3)
                    features(s, 3, 1, 0, wide[1 - s.par(3)], s_ck)
                if s.active(5):
                    pe.wait_ge(s_xn2, 2 * b5 + 2)
                    wait(pe, s_lo, 2 * done(b2 + 1))
                    wait(pe, s_ysb, b5)
                    for t in range(NT):
                        mm = pe.transpose(m0[:, t * P:(t + 1) * P], xn2[:, t, :], ident)
                    mm.then_inc(s_x2t, 1)
                if s.active(4):
                    pe.wait_ge(s_kvb, b4 + 1)
                    pe.wait_ge(s_expq, 2 * b4 + 2)
                    for n in range(NP):
                        c, r = n % 4, n // 4
                        mm = pe.matmul(m1[c * PW:(c + 1) * PW, r * N:(r + 1) * N], kvb[:, n, :], eq_t[:, n, :],
                                       start=(r == 0), stop=True, tile_position=(0, c * PW),
                                       skip_group_check=True)
                    mm.then_inc(s_out, 1)
                if s.active(2):
                    pe.wait_ge(s_xnt, b2 + 1)
                    wait(pe, s_xn2t, b5 + 1)
                    wait(pe, s_lo, 2 * (b2 + 1))
                    for t in range(NT):
                        mm = pe.matmul(m0[:, t * D:(t + 1) * D], xn_t[:, t * P:(t + 1) * P], wv_t[:, :],
                                       start=True, stop=True)
                    mm.then_inc(s_v, 1)
                if s.active(5):
                    pe.wait_ge(s_xn2t, b5 + 1)
                    wait(pe, s_maxq, 2 * done(b3 + 1))
                    wait(pe, s_expq, 2 * done(b4 + 1))
                    for c in range(FC):
                        mm = pe.matmul(wide[2][:, c * N:(c + 1) * N], wfc_t[:, c, :], xn2_t[:, :],
                                       start=True, stop=True)
                    mm.then_inc(s_ff1, 1)
                if s.active(4):
                    pe.wait_ge(s_outt, 2 * b4 + 2)
                    for t in range(NT):
                        for r in range(NR):
                            c = (t * NR + r) * P
                            mm = pe.transpose(m1[:, c:c + P], out_t[:, r, t * P:(t + 1) * P], ident)
                    mm.then_inc(s_trout, 1)
                if s.active(3):
                    pe.wait_ge(s_spq, 4 * b3 + 4)
                    wait(pe, s_vsb, 2 * done(b2 + 1))
                    wait(pe, s_xn2t, b5 + 1)
                    for t in range(NT):
                        mm = pe.transpose(m0[:, t * P // 2:(t + 1) * P // 2].bitcast(BF16), parts_q[:, t, :],
                                          ident_bf[:, :])
                    mm.then_inc(s_ptq, 1)
                    pe.wait_ge(s_maxq, 2 * b3 + 1)
                    features(s, 3, 1, 1, wide[s.par(3)], s_ck)
                    pe.wait_ge(s_spk, 8 * b3 + 4)
                    wait(pe, s_ptq_sb, b3 + 1)
                    parts_k_t(m0, 0)
                if s.active(4):
                    pe.wait_ge(s_att, b4 + 1)
                    for t in range(NT):
                        mm = pe.transpose(m1[:, t * P:(t + 1) * P],
                                          att[:, t * H:(t + 1) * H, :].rearrange("p h d -> p (h d)"), ident)
                    mm.then_inc(s_attt, 1)
                if s.active(3):
                    pe.wait_ge(s_ptq_sb, b3 + 1)
                    wait(pe, s_relu, b5 + 1)
                    wait(pe, s_maxq, 2 * (b3 + 1))
                    features_t(s, 3, 0)
                if s.active(4):
                    pe.wait_ge(s_attt_sb, b4 + 1)
                    for t in range(NT):
                        mm = pe.matmul(m1[:, t * D:(t + 1) * D], att_t[:, t * P:(t + 1) * P], wp_t[:, :],
                                       start=True, stop=True)
                    mm.then_inc(s_proj, 1)
                if s.active(5):
                    pe.wait_ge(s_hsq, b5 + 1)
                    wait(pe, s_ptk_sb, 2 * done(b3 + 1) - 1)
                    wait(pe, s_xn2t, b5 + 1)
                    for t in range(NT):
                        for c in range(FC):
                            mm = pe.matmul(m0[:, t * D:(t + 1) * D], hsq[:, c, t * P:(t + 1) * P],
                                           wpr_t[:, c, :], start=(c == 0), stop=(c == FC - 1))
                    mm.then_inc(s_y, 1)

            slots(pe, body)

        @block.vector
        def _(dve):
            dve.wait_ge(s_first, 16 * N_FIRST)
            dve.tensor_copy(pm16[:, :, :], pm_raw[:, :].unsqueeze(1).broadcast_to([M, 4 * HG, HD])).then_inc(s_pmrep, 1)

            def stacked_projection():
                dve.wait_ge(s_wtr, 2)
                for j in range(HG):
                    dve.tensor_scalar(pf[:, j, :], wide[0][:, 512:512 + M], head_mask[:, j:j + 1], SPLIT_SCALE, ALU.mult,
                                      ALU.mult).then_inc(s_pmrep, 1)
                dve.wait_ge(s_pmrep, 1 + HG)
                dve.tensor_copy(pf_hi[:, :, :], pf[:, :, :]).then_inc(s_pmrep, 1)
                dve.wait_ge(s_pmrep, 2 + HG)
                dve.tensor_tensor(pf_lo[:, :, :], pf[:, :, :], pf_hi[:, :, :], ALU.subtract).then_inc(s_pmrep, 1)
                dve.tensor_scalar(pst_a[:, :], pf_hi[:, :, :].rearrange("p h m -> p (h m)"),
                                  cst[:, P + HG:P + HG + 1], None, ALU.mult).then_inc(s_pmrep, 1)
                dve.wait_ge(s_pmrep, 4 + HG)
                dve.scalar_tensor_tensor(pst[:, :], pf_lo[:, :, :].rearrange("p h m -> p (h m)"),
                                         cst[:, P + HG + 1:P + HG + 2], pst_a[:, :], ALU.mult,
                                         ALU.add).then_inc(s_prep, 1)
                dve.wait_ge(s_const, 16 * N_CONST)

            def stats(k, b, tiles, ready):
                for sm, value in ready:
                    wait(dve, sm, value)
                wait(dve, s_mv[k], 2 * b)
                for t in range(NT):
                    dve.bn_stats(st[k][:, t, :], tiles[t]).then_inc(s_stat[k], 1)
                wait(dve, s_rstd[k], b)
                dve.wait_ge(s_stat[k], 2 * b + 2)
                settle(dve)
                for t in range(NT):
                    dve.bn_aggr(mv[k][:, t, :], st[k][:, t, :]).then_inc(s_mv[k], 1)

            def maxima(w, nm, t, s_done):
                dve.tensor_reduce(nm[:, t, :], w[:, :].rearrange("p (h m) -> p h m", h=H), AX_X, ALU.max,
                                  negate=True).then_inc(s_done, 1)

            def body(s):
                b0, b1, b2, b3, b4, b5 = (s.seq(k) for k in range(6))
                if s.active(3):
                    wait(dve, s_spq, 4 * b3)
                    dve.wait_ge(s_cq, 2 * b3 + 1)
                    maxima(wide[s.par(3)], nmax_q, 0, s_maxq)
                    dve.wait_ge(s_cq, 2 * b3 + 2)
                    maxima(wide[2], nmax_q, 1, s_maxq)
                if s.active(4):
                    dve.wait_ge(s_kvt, 2 * b4 + 2)
                    wait(dve, s_outt, 2 * b4)
                    dve.tensor_scalar(kv_sum8[:, :], kv_sum[:, :], EPS8, None, ALU.mult).then_inc(s_kvsum, 1)
                if s.active(3):
                    wait(dve, s_spk, 8 * b3)
                    dve.wait_ge(s_ck, 2 * b3 + 1)
                    maxima(wide[1 - s.par(3)], nmax_k, 0, s_maxk)
                if s.active(2):
                    p = s.par(2)
                    dve.wait_ge(s_v, b2 + 1)
                    wait(dve, s_kv, b2 - 1)
                    for h in range(2):
                        dve.tensor_tensor(vaug[p][:, :, :, h * VW:h * VW + HD],
                                          m0[:, 0:NT * D].rearrange("p (t n d) -> p t n d", t=NT, n=NP)
                                          [:, :, :, h * HD:(h + 1) * HD],
                                          bv[:, :, :].rearrange("p t (n d) -> p t n d", n=NP)
                                          [:, :, :, h * HD:(h + 1) * HD], ALU.add).then_inc(s_vsb, 1)
                if s.active(4):
                    dve.wait_ge(s_trout, b4 + 1)
                    o = m1[:, :].rearrange("p (n c) -> p n c", c=PW)[:, :, 0:2 * VW].rearrange(
                        "p n (h c) -> p n h c", h=2)
                    dve.tensor_scalar(den[:, :].rearrange("p (n h) -> p n h", h=2), o[:, :, :, HD],
                                      64.0 * EPS_FAVOR, None, ALU.add).then_inc(s_den, 1)
                    dve.wait_ge(s_den, b4 + 1)
                    dve.reciprocal(rden[:, :], den[:, :]).then_inc(s_rden, 1)
                    dve.wait_ge(s_rden, b4 + 1)
                    wait(dve, s_attt, b4)
                    dve.tensor_tensor(att[:, :, :].rearrange("p (n h) d -> p n h d", h=2), o[:, :, :, 0:HD],
                                      rden[:, :].rearrange("p (n h) -> p n h", h=2).unsqueeze(3)
                                      .broadcast_to([P, NT * NP, 2, HD]), ALU.mult).then_inc(s_att, 1)
                if s.active(3):
                    dve.wait_ge(s_ck, 2 * b3 + 2)
                    maxima(wide[s.par(3)], nmax_k, 1, s_maxk)
                if s.active(4):
                    dve.wait_ge(s_proj, b4 + 1)
                    wait(dve, s_x1n, 2 * b4)
                    dve.tensor_tensor(a_sb[:, :, :], m1[:, 0:NT * D].rearrange("p (t d) -> p t d", t=NT),
                                      bp[:, :, :], ALU.add).then_inc(s_a, 1)
                    stats(1, b4, [a_sb[:, t, :] for t in range(NT)], [(s_a, b4 + 1)])
                if s.active(0):
                    p = s.par(0)
                    stats(0, b0, [xin[p][:, t, :] for t in range(NT)], [(s_xin[p], 16 * (s.round(0) + 1))])
                if s.first(1):
                    stacked_projection()
                if s.active(5):
                    dve.wait_ge(s_ysb, b5 + 1)
                    wait(dve, s_cn, 2 * b5)
                    for n in range(NUM_STEPS):
                        for t in range(NT):
                            dst, last = (cnt[(n + i) % 2][:, t * D:(t + 1) * D] for i in range(2))
                            y = y_sb[:, t * D:(t + 1) * D]
                            if n == 0:
                                dve.tensor_scalar(dst, y, thresholds[0], None, ALU.is_gt).then_inc(s_cnt, 1)
                            else:
                                dve.wait_ge(s_cnt, NT * (NUM_STEPS * b5 + n - 1) + t + 1)
                                dve.scalar_tensor_tensor(dst, y, thresholds[n], last, ALU.is_gt,
                                                         ALU.add).then_inc(s_cnt, 1)
                if s.active(4):
                    stats(2, b4, [x1[s.par(4)][:, t, :] for t in range(NT)], [(s_x1, b4 + 1)])
                if s.active(5):
                    stats(3, b5, [cnt[0][:, t * D:(t + 1) * D] for t in range(NT)],
                          [(s_cnt, NT * NUM_STEPS * (b5 + 1))])
                if s.active(1):
                    dve.wait_ge(s_hi, 2 * b1 + 2)
                    for j in range(2):
                        dve.scalar_tensor_tensor(lo[:, j, :], m0[:, j * N:(j + 1) * N], bq[:, j:j + 1],
                                                 hi[:, j, :], ALU.add, ALU.subtract).then_inc(s_lo, 1)
                if s.active(3):
                    dve.wait_ge(s_kv, b3 + 1)
                    wait(dve, s_trkv, b3)
                    for r in range(NR):
                        dve.scalar_tensor_tensor(kvt[:, r, :], m1[:, r * MW:r * MW + 2 * M],
                                                 m1[:, r * MW + 2 * M:(r + 1) * MW], kv_mask, ALU.add, ALU.mult,
                                                 accum_out=kv_sum[:, r:r + 1]).then_inc(s_kvt, 1)

            slots(dve, body)


_INS = ['L0_attn_x', 'L0_attn_qkv_w', 'L0_attn_qkv_b', 'L0_attn_proj_w', 'L0_attn_proj_b',
        'L0_attn_projection_matrix', 'L0_ffn_W_fc', 'L0_ffn_W_proj']


def kernel(**inputs):
    import numpy as _np
    import concourse.bacc as _bacc
    from concourse import mybir as _mybir
    from concourse.bass_utils import run_bass_kernel_spmd as _run

    rows = _np.arange(128)
    const = _np.zeros((128, 128 + 4 + 2 + 128), _np.float32)
    const[rows, rows] = 1
    const[rows, 128 + rows % 32 // 8] = 1
    const[rows, 132 + rows // 32 % 2] = 1
    for head in range(2):
        const[rows % 32 // 9 == head, 134 + 64 * head:134 + 64 * (head + 1)] = 1
    indicator = _np.zeros((128, 16, 64), _np.float16)
    for part in range(3):
        indicator[16 * part + _np.arange(16), _np.arange(16)] = 1

    nc = _bacc.Bacc("TRN2", target_bir_lowering=False, num_devices=1)
    arrays, args = {}, []
    named = {**{name: inputs[name] for name in _INS}, "const": const, "indicator": indicator.reshape(128, 1024)}
    for name, value in named.items():
        a = _np.ascontiguousarray(value)
        arrays[f"in_{name}_dram"] = a
        args.append(nc.dram_tensor(f"in_{name}_dram", a.shape, _mybir.dt.from_np(a.dtype), kind="ExternalInput").ap())
    shape = inputs["L0_attn_x"].shape
    args.append(nc.dram_tensor("out_0_dram", shape, _mybir.dt.float32, kind="ExternalOutput").ap())
    sandwich_kernel(nc, *args)
    r = _run(nc, [arrays], core_ids=[0])
    return r.results[0]["out_0_dram"]
```
